# Optimizing a Trainium2 kernel written in Bass

```python
import numpy as np
import jax
import jax.numpy as jnp

def _softmax(x, axis=-1):
    return jax.nn.softmax(x, axis=axis)

def _gelu(x):
    return jax.nn.gelu(x, approximate=True)

def _silu(x):
    return jax.nn.silu(x)

def _sigmoid(x):
    return jax.nn.sigmoid(x)

def _layernorm(x, axis=-1, eps=1e-05):
    m = jnp.mean(x, axis=axis, keepdims=True)
    v = jnp.var(x, axis=axis, keepdims=True)
    return (x - m) / jnp.sqrt(v + eps)

def _scatter_add(tgt, idx, src, axis=0):
    return tgt.at[idx].add(src)

def _segment_sum(src, seg, n):
    return jax.ops.segment_sum(src, seg, n)
kernel_name = 'mk_gnn_ffn_d1_gnn_r64_51fdfd'

def setup_inputs(seed: int=0):
    np.random.seed(seed)
    _w = jnp.asarray

    def _rec_inputs():
        import jax
        import jax.numpy as jnp
        _gk = jax.random.key(seed)
        x = -0.0003713 + 1 * jax.random.normal(jax.random.fold_in(_gk, 1), (50000, 256), jnp.float32)
        _s = jax.random.randint(jax.random.fold_in(_gk, 2), (6250,), 0, 50000, jnp.int32)
        _d = jax.random.randint(jax.random.fold_in(_gk, 3), (6250,), 0, 50000, jnp.int32)
        _loop = jnp.arange(50000, dtype=jnp.int32)
        src = jnp.concatenate([_s, _d, _loop])
        dst = jnp.concatenate([_d, _s, _loop])
        _o = jnp.argsort(dst, stable=True)
        src = src[_o]
        dst = dst[_o]
        return (x, src, dst)
    x, src, dst = _rec_inputs()

    def _L0_gnn_setup():
        import jax, jax.numpy as jnp
        import numpy as np
        N = 50000
        E = 12500
        HIDDEN = 256
        HEADS = 8
        HEAD_DIM = HIDDEN // HEADS

        def _linear_params(key, fan_in, fan_out):
            k1, k2 = jax.random.split(key)
            s = 1.0 / np.sqrt(fan_in)
            W = jax.random.uniform(k1, (fan_in, fan_out), jnp.float32, -s, s)
            b = jax.random.uniform(k2, (fan_out,), jnp.float32, -s, s)
            return (W, b)
        key = jax.random.key(seed)
        ks = jax.random.split(key, 7)
        h = jax.random.normal(ks[0], (N, HIDDEN), jnp.float32)
        row = jnp.sort(jax.random.randint(ks[1], (E,), 0, N))
        col = jax.random.randint(ks[2], (E,), 0, N)
        Wq, bq = _linear_params(ks[3], HIDDEN, HIDDEN)
        Wk, bk = _linear_params(ks[4], HIDDEN, HIDDEN)
        Wv, bv = _linear_params(ks[5], HIDDEN, HIDDEN)
        Wo, bo = _linear_params(ks[6], HIDDEN, HIDDEN)
        return dict(h=h, row=row, col=col, Wq=Wq, bq=bq, Wk=Wk, bk=bk, Wv=Wv, bv=bv, Wo=Wo, bo=bo)
    _L0_gnn_all = _L0_gnn_setup()
    _L0_gnn_in = {k: v for k, v in _L0_gnn_all.items() if k in ('Wq', 'bq', 'Wk', 'bk', 'Wv', 'bv', 'Wo', 'bo')}
    del _L0_gnn_all

    def _L0_ffn_setup():
        import jax, jax.numpy as jnp
        import numpy as np
        B, S, D = (8, 64, 256)
        H = 4 * D
        CAPACITY = 0.5
        key = jax.random.key(seed)
        ks = jax.random.split(key, 6)
        x = jax.random.normal(ks[0], (B, S, D), dtype=jnp.float32)
        attention_mask = jnp.zeros((B, 1, 1, S), dtype=jnp.float32)
        wr = jax.random.normal(ks[1], (D, 1), dtype=jnp.float32) * 0.02
        br = jnp.zeros((1,), dtype=jnp.float32)
        w1 = jax.random.normal(ks[2], (D, H), dtype=jnp.float32) * 0.02
        b1 = jnp.zeros((H,), dtype=jnp.float32)
        w2 = jax.random.normal(ks[3], (H, D), dtype=jnp.float32) * 0.02
        b2 = jnp.zeros((D,), dtype=jnp.float32)
        return {'x': x, 'attention_mask': attention_mask, 'wr': wr, 'br': br, 'w1': w1, 'b1': b1, 'w2': w2, 'b2': b2}
    _L0_ffn_all = _L0_ffn_setup()
    _L0_ffn_in = {k: v for k, v in _L0_ffn_all.items() if k in ('attention_mask', 'wr', 'br', 'w1', 'b1', 'w2', 'b2')}
    del _L0_ffn_all
    return {'x': x, 'src': src, 'dst': dst, 'L0_gnn_Wq': _L0_gnn_in['Wq'], 'L0_gnn_bq': _L0_gnn_in['bq'], 'L0_gnn_Wk': _L0_gnn_in['Wk'], 'L0_gnn_bk': _L0_gnn_in['bk'], 'L0_gnn_Wv': _L0_gnn_in['Wv'], 'L0_gnn_bv': _L0_gnn_in['bv'], 'L0_gnn_Wo': _L0_gnn_in['Wo'], 'L0_gnn_bo': _L0_gnn_in['bo'], 'L0_ffn_attention_mask': _L0_ffn_in['attention_mask'], 'L0_ffn_wr': _L0_ffn_in['wr'], 'L0_ffn_br': _L0_ffn_in['br'], 'L0_ffn_w1': _L0_ffn_in['w1'], 'L0_ffn_b1': _L0_ffn_in['b1'], 'L0_ffn_w2': _L0_ffn_in['w2'], 'L0_ffn_b2': _L0_ffn_in['b2']}

def reference(x, src, dst, L0_gnn_Wq, L0_gnn_bq, L0_gnn_Wk, L0_gnn_bk, L0_gnn_Wv, L0_gnn_bv, L0_gnn_Wo, L0_gnn_bo, L0_ffn_attention_mask, L0_ffn_wr, L0_ffn_br, L0_ffn_w1, L0_ffn_b1, L0_ffn_w2, L0_ffn_b2):
    import jax
    import jax.numpy as jnp

    def _L0_gnn_ref(h, row, col, Wq, bq, Wk, bk, Wv, bv, Wo, bo):
        import jax, jax.numpy as jnp
        import numpy as np
        N = 50000
        E = 12500
        HIDDEN = 256
        HEADS = 8
        HEAD_DIM = HIDDEN // HEADS

        def _linear_params(key, fan_in, fan_out):
            k1, k2 = jax.random.split(key)
            s = 1.0 / np.sqrt(fan_in)
            W = jax.random.uniform(k1, (fan_in, fan_out), jnp.float32, -s, s)
            b = jax.random.uniform(k2, (fan_out,), jnp.float32, -s, s)
            return (W, b)
        n = h.shape[0]
        scaling = HEAD_DIM ** (-0.5)
        q = (h @ Wq + bq).reshape(n, HEADS, HEAD_DIM) * scaling
        k = (h @ Wk + bk).reshape(n, HEADS, HEAD_DIM)
        v = (h @ Wv + bv).reshape(n, HEADS, HEAD_DIM)
        s = jnp.einsum('ehd,ehd->eh', q[row], k[col])
        m = jax.ops.segment_max(s, row, num_segments=n)
        p = jnp.exp(s - m[row])
        denom = jax.ops.segment_sum(p, row, num_segments=n)
        attn = p / denom[row]
        out = jax.ops.segment_sum(attn[:, :, None] * v[col], row, num_segments=n)
        return out.reshape(n, HIDDEN) @ Wo + bo

    def _L0_ffn_ref(x, attention_mask, wr, br, w1, b1, w2, b2):
        import jax, jax.numpy as jnp
        import numpy as np
        B, S, D = (8, 64, 256)
        H = 4 * D
        CAPACITY = 0.5
        b, s, d = x.shape
        weights = (jnp.einsum('bsd,do->bso', x, wr) + br)[..., 0]
        k = max(1, int(CAPACITY * s))
        kk = k - 1 if k > 1 else 1
        _, idx = jax.lax.top_k(weights, k)
        sel_idx = idx[:, :kk]
        sel = jnp.take_along_axis(x, sel_idx[:, :, None], axis=1)
        h = jax.nn.gelu(jnp.einsum('bkd,dh->bkh', sel, w1) + b1)
        y = jnp.einsum('bkh,hd->bkd', h, w2) + b2
        w_sel = jnp.take_along_axis(weights, sel_idx, axis=1)
        y = y * w_sel[..., None]
        batch_idx = jnp.arange(b)[:, None]
        processed = jnp.zeros_like(x).at[batch_idx, sel_idx].set(y)
        return processed + x
    x = x + _L0_gnn_ref(_layernorm(x, axis=-1), src, dst, L0_gnn_Wq, L0_gnn_bq, L0_gnn_Wk, L0_gnn_bk, L0_gnn_Wv, L0_gnn_bv, L0_gnn_Wo, L0_gnn_bo)
    x = x + _L0_ffn_ref(_layernorm(x, axis=-1)[None], L0_ffn_attention_mask, L0_ffn_wr, L0_ffn_br, L0_ffn_w1, L0_ffn_b1, L0_ffn_w2, L0_ffn_b2)[0]
    return x

_drawn_inputs = setup_inputs


def setup_inputs(seed=0):
    import zlib

    import numpy as np

    out = dict(_drawn_inputs(seed))
    spreads = {'L0_ffn_b1': (0.0, 0.8), 'L0_ffn_b2': (0.0, 0.741)}
    factors = {'L0_gnn_bq': 30.901,
     'L0_gnn_bk': 64.0,
     'L0_gnn_bv': 3.037,
     'L0_ffn_wr': 3.944,
     'L0_ffn_w1': 4.655,
     'L0_ffn_w2': 4.342}
    for name, (base, spread) in spreads.items():
        noise = np.random.default_rng([zlib.crc32(name.encode()), seed]).standard_normal(out[name].shape)
        drawn = base * np.exp(spread * noise) if base else spread * noise
        out[name] = jnp.asarray(drawn.astype(out[name].dtype))
    for name, factor in factors.items():
        out[name] = (out[name] * factor).astype(out[name].dtype)
    return out
```

```python
import concourse.bass as bass
from concourse import mybir
from concourse.alu_op_type import AluOpType as ALU
from contextlib import ExitStack

f32 = mybir.dt.float32
bf16 = mybir.dt.bfloat16
i32 = mybir.dt.int32
i16 = mybir.dt.int16
u16 = mybir.dt.uint16
ACT = mybir.ActivationFunctionType
AX = mybir.AxisListType.X
IDX = bass.IndirectOffsetOnAxis
ds = bass.ds

P = 128
D = 256
HEADS = 8
HD = D // HEADS
HID = 4 * D
EPS = 1e-5
BIG = 1e30
NONE = 65535
FAR = 70000.0


def gnn_ffn_kernel(nc, x, src, dst, Wq, bq, Wk, bk, Wv, bv, Wo, bo, wr, br, w1, b1, w2, b2, out):
    N = x.shape[0]
    E = src.shape[0]
    T = N // P
    REST = N - P * T
    G = 3
    NGRP = T // G
    assert T % (2 * G) == 0 and 0 < REST and REST % 16 == 0
    TC = T + G
    LO = 512
    HI = (N + LO - 1) // LO
    EP = 125
    EC = E // EP
    assert E == EP * EC and EC % 20 == 0
    JC = (-(-E // P) + 7) // 8 * 8
    JB = JC // 4
    assert JB <= P and JC <= 512
    LBASE = P
    LLEN = JC * P + 2 * P
    KK = max(1, N // 2) - 1
    FG = 4
    NFG = -(-KK // (FG * P))
    FC = NFG * FG
    KT = D // P
    HT = HID // P
    SCALE = HD ** -0.5

    qkv_t = nc.dram_tensor("qkv_t", [N, 3 * D], f32, kind="Internal").ap()
    attn_t = nc.dram_tensor("attn_t", [N, D], f32, kind="Internal").ap()
    cnt_t = nc.dram_tensor("cnt_t", [HI * LO, 1], f32, kind="Internal").ap()
    seen_t = nc.dram_tensor("seen_t", [HI * LO, 1], f32, kind="Internal").ap()
    lists = [nc.dram_tensor(f"list_{k}", [LLEN, 2], i32, kind="Internal").ap() for k in range(2)]
    reset_t = nc.dram_tensor("reset_t", [JC, P], f32, kind="Internal").ap()
    norm_t = nc.dram_tensor("norm_t", [N, 4], f32, kind="Internal").ap()

    def grouped(table, w):
        return table[0:P * T, :].rearrange("(p t) c -> p t c", t=T)

    with ExitStack() as ctx:
        def sb(name, shape, dt=f32):
            return ctx.enter_context(nc.sbuf_tensor(name, shape, dt))

        def sem(name):
            return ctx.enter_context(nc.semaphore(name))

        def pair(name):
            return [sem(f"{name}{u}") for u in range(2)]

        wqkv = sb("wqkv", [P, KT, 3 * D])
        wo = sb("wo", [P, KT, D])
        w1s = sb("w1s", [P, KT, HID])
        w2s = sb("w2s", [P, HT, D])
        bqkv = sb("bqkv", [P, 3 * D])
        bos = sb("bos", [P, D])
        b2s = sb("b2s", [P, D])
        b1s = sb("b1s", [P, HT])
        wrs = sb("wrs", [P, D])
        brs = sb("brs", [P, 1])
        ident = sb("ident", [P, P])
        iota = sb("iota", [P, LO], i16)
        digits = sb("digits", [P, 16])
        bits = sb("bits", [P, 16])
        from_here = sb("from_here", [P, P], bf16)
        ones_b = sb("ones_b", [P, P], bf16)
        zeros_b = sb("zeros_b", [P, LO], bf16)
        before = sb("before", [P, P])
        ones = sb("ones", [P, P])
        zeros = sb("zeros", [P, LO])
        eps = sb("eps", [P, 1])
        opened = sb("opened", [16, 16, 16])
        node = sb("node", [P, TC], i32)

        SPACE = 18432
        space = sb("space", [P, SPACE])
        taken = {"early": 0, "late": 0}

        def in_space(when, shape, dt=f32, each=1):
            width = 1
            for n in shape[1:]:
                width *= n
            a = taken[when]
            taken[when] += (width + each - 1) // each
            assert taken[when] <= SPACE
            v = space[0:shape[0], a:taken[when]]
            if dt != f32:
                v = v.bitcast(dt)[:, 0:width]
            names = "abc"[0:len(shape) - 1]
            if len(names) > 1:
                sizes = {n: c for n, c in zip(names, shape[1:])}
                v = v.rearrange(f"p ({' '.join(names)}) -> p {' '.join(names)}", **sizes)
            return v

        def early(*shape, dt=f32, each=1):
            return in_space("early", shape, dt, each)

        def late(*shape, dt=f32, each=1):
            return in_space("late", shape, dt, each)

        bank = [ctx.enter_context(nc.psum_tensor(f"qkv_ps{k}", [P, 1024], f32)) for k in range(2)]
        bank2 = [ctx.enter_context(nc.psum_tensor(f"ps{k}", [P, 512], f32)) for k in range(4)]
        qkv_ps = bank
        tp_ps = bank2[0:2]
        sort_ps = bank2[2:4]
        half = [bank[0][:, 0:512], bank[0][:, 512:1024], bank[1][:, 0:512], bank[1][:, 512:1024]]

        none = early(P, LLEN * 2 // P, dt=i32)
        edge = early(EP, 2, EC, dt=i32)
        edge_f = early(EP, 2, EC)
        is_self = early(EP, EC)
        lo_i = early(EP, EC, dt=i32)
        hi_i = early(EP, EC, dt=i32)
        lo_f = early(EP, EC)
        hi_f = early(EP, EC)
        oh_hi = early(EP, 4, P, dt=bf16, each=2)
        oh_lo = early(EP, 4, LO, dt=bf16, each=2)
        cnt_s = early(HI, LO)
        W = max(EC, JC)
        digit_i = early(P, W, dt=i32)
        digit = early(P, W)
        onehot = early(P, W, dt=bf16, each=2)
        upto = early(P, W)
        place = early(P, W)
        pos = early(P, W)
        pos_i = early(P, W, dt=i32)
        base = sb("base", [P, 1])
        pay = early(P, W, 2, dt=i32)
        row_i = early(P, JC, dt=i32)
        idx_blk = sb("idx_blk", [P, 2, 10], i32)
        pay_blk = sb("pay_blk", [P, 2, 10, 2], i32)
        groups_f = sb("groups_f", [P, 1])
        groups_i = sb("groups_i", [P, 1], i32)
        lst = early(JB, 4, 2 * P, dt=i32)
        lst_f = early(JB, 2, 4, P)
        near = early(JB, 2, 4, 2 * P, dt=i32)
        near_f = early(JB, 2, 4, P)
        reset_s = early(JB, 4, P)

        rows_in = sb("rows_in", [P, 4, G, D])
        xg, ag = rows_in[:, 0:2, :, :], rows_in[:, 2:4, :, :]
        stats = sb("stats", [P, 2, G, 6])
        mv = sb("mv", [P, 2, G, 2])
        sd = sb("sd", [P, 2, G])
        rs = sb("rs", [P, 2, G])
        h = sb("h", [P, 2, G, D])
        ht = sb("ht", [P, 2, G, D])
        qkv = sb("qkv", [P, 2, G, 3 * D])

        col_row = sb("col_row", [P, JC + 2])
        col_last = sb("col_last", [P, JC + 2])
        col_carry = sb("col_carry", [P, JC + 2])
        col_next = sb("col_next", [P, JC + 2])
        idx_all = sb("idx_all", [P, JC + 2, 3], i32)
        gidx = sb("gidx", [P, 2, 3], i32)
        sidx = sb("sidx", [P, 2, 1], i32)
        ends = sb("ends", [P, 4, 3 * D])
        rowg, colg = ends[:, 0:2, :], ends[:, 2:4, :]
        cntg = sb("cntg", [P, 2, 1])
        row_bc = sb("row_bc", [P, 2, P, 2], i32)
        reset_bc = sb("reset_bc", [HEADS, 2, P])
        qk = sb("qk", [P, 2, D])
        same = sb("same", [P, P])
        lastm = sb("lastm", [P, P])
        carrym = sb("carrym", [P, P])
        no_self = sb("no_self", [P, 1])
        raw = sb("raw", [P, 2, HEADS])
        sc = sb("sc", [P, 2, HEADS])
        smax = sb("smax", [P, HEADS])
        run = sb("run", [HEADS, 2, P])
        runt = sb("runt", [P, HEADS])
        expo = sb("expo", [P, 3, HEADS])
        ex = sb("ex", [P, 3, HEADS])
        pv = sb("pv", [P, D + HEADS])
        selfv = sb("selfv", [P, D])
        selfw = sb("selfw", [P, HEADS])
        carried = sb("carried", [P, D + HEADS])
        state = sb("state", [P, 2, HEADS + D + HEADS])
        tot = sb("tot", [P, D])
        totw = sb("totw", [P, HEADS])
        outb = sb("outb", [P, 2, D])

        fh = late(P, 2, HT, FG * P)
        after_fh, taken["late"] = taken["late"], 0
        xb = late(P, 2, G, D)
        x1 = late(P, 2, G, D)
        ug = late(P, 2, G, D)
        zt = late(P, G, D)
        taken["late"] = after_fh
        shift = sb("shift", [P, 2, G])
        gain = sb("gain", [P, 2, G])
        wst = sb("wst", [P, 2, G])
        cnt_n = sb("cnt_n", [P, TC])
        seen_n = sb("seen_n", [P, TC])
        has = late(P, TC)
        mean_n = late(P, TC)
        rs_n = late(P, TC)
        weight = late(P, TC)
        norm_s = late(P, TC, 4)

        key_a = late(P, T + 1, dt=i32)
        key_b = late(P, T + 1, dt=i32)
        key = late(P, 2, T + 1)
        keyl = late(P, T + 1)
        hit = late(P, T + 1)
        tied = late(P, T + 1)
        rank = late(P, T + 1)
        chpos = late(P, T + 1, dt=i32)
        thr = sb("thr", [P, 2])
        cand = sb("cand", [P, 1])
        cntc = sb("cntc", [P, 1])
        step = sb("step", [P, 1])
        need = sb("need", [P, 1])
        off = sb("off", [P, 2])
        live = sb("live", [P, 1])
        pcol = sb("pcol", [P, 1])
        off1 = sb("off1", [P, 1])
        slot_f = late(P, 2, T + 1)
        node_f = late(P, 2, T + 1)
        oh_slot = late(P, 4, 2, P, dt=bf16, each=2)
        oh_col = late(P, 4, FC, dt=bf16, each=2)
        past = late(P, FC)

        chosen = late(P, FC, dt=i32)
        fidx = sb("fidx", [P, 2, FG], i32)
        fu = rows_in[:, :, :, :].rearrange("p a b c -> p (a b c)")[:, 0:2 * FG * D]\
            .rearrange("p (u c d) -> p u c d", u=2, c=FG)
        fn = sb("fn", [P, 2, FG, 4])
        spent = qkv[:, :, :, :].rearrange("p a b c -> p (a b c)")
        fz, fo = (spent[:, k * 2 * FG * D:(k + 1) * 2 * FG * D].rearrange("p (u c d) -> p u c d", u=2, c=FG)
                  for k in range(2))
        fzt = ends[:, :, :].rearrange("p a c -> p (a c)")[:, 0:2 * KT * FG * P]\
            .rearrange("p (u k n) -> p u k n", u=2, k=KT)
        fy = late(P, 2, D)

        consts = sem("consts")
        aside = sem("aside")
        iota_ready = sem("iota_ready")
        edges_in = sem("edges_in")
        wqkv_in = sem("wqkv_in")
        late_in = sem("late_in")
        prefilled = sem("prefilled")
        hist_oh = sem("hist_oh")
        hist_free = sem("hist_free")
        hist_done = sem("hist_done")
        cnt_ready = sem("cnt_ready")
        cnt_stored = sem("cnt_stored")
        sort_oh = sem("sort_oh")
        sort_mm = sem("sort_mm")
        pos_ready = sem("pos_ready")
        groups_ready = sem("groups_ready")
        scat = [pair(f"scat{k}_") for k in range(4)]
        scattered = sem("scattered")
        list_in = sem("list_in")
        list_f = sem("list_f")
        list_t = sem("list_t")
        reset_ready = sem("reset_ready")
        reset_stored = sem("reset_stored")
        cols_ready = sem("cols_ready")

        ax_in = pair("ax_in")
        a_var = sem("a_var")
        a_sd = sem("a_sd")
        a_h = sem("a_h")
        a_tp = sem("a_tp")
        a_ht = sem("a_ht")
        a_mm = sem("a_mm")
        a_ev = sem("a_ev")
        a_stored = pair("a_stored")

        e_row_in = pair("e_row_in")
        e_in = pair("e_in")
        e_smax = sem("e_smax")
        e_st = sem("e_st")
        e_run = sem("e_run")
        e_rt = sem("e_rt")
        e_runt = sem("e_runt")
        e_max = sem("e_max")
        e_cmax = sem("e_cmax")
        e_expo = sem("e_expo")
        e_ex = sem("e_ex")
        e_pv = sem("e_pv")
        e_sum = sem("e_sum")
        e_state = sem("e_state")
        e_out = pair("e_out")
        e_sc = pair("e_sc")
        e_end = sem("e_end")

        has_in = sem("has_in")
        b_in = pair("b_in")
        b_xb = sem("b_xb")
        b_tp = sem("b_tp")
        b_at = sem("b_at")
        b_mm = sem("b_mm")
        b_x1 = sem("b_x1")
        b_x1t = sem("b_x1t")
        b_var = sem("b_var")
        b_sd = sem("b_sd")
        b_gain = sem("b_gain")
        b_u = sem("b_u")
        b_fin = sem("b_fin")
        b_stored = pair("b_stored")

        t_cnt = sem("t_cnt")
        t_sum = sem("t_sum")
        norm_ready = sem("norm_ready")
        norm_stored = sem("norm_stored")
        ch_oh = sem("ch_oh")
        ch_free = sem("ch_free")
        ch_done = sem("ch_done")
        ch_ready = sem("ch_ready")

        f_in = pair("f_in")
        f_z = sem("f_z")
        f_tp = sem("f_tp")
        f_zt = sem("f_zt")
        f_m1 = sem("f_m1")
        f_h = sem("f_h")
        f_m2 = sem("f_m2")
        f_y = sem("f_y")
        f_o = sem("f_o")
        f_sc = pair("f_sc")

        cuts = [0, NGRP // 2 * 34 // 65, NGRP // 2 * 43 // 65, NGRP // 2 * 52 // 65]
        block = ctx.enter_context(nc.Block())

        @block.sync
        def _(sp):
            for k, s in enumerate((*a_stored, *b_stored)):
                sp.dma_start(opened[:, k, :], x[0:16, 0:16]).then_inc(s, 16)
            for k, e in enumerate((src, dst)):
                sp.dma_start(edge[:, k, :], e.rearrange("(p c) -> p c", c=EC)).then_inc(edges_in, 16)
            for k, w in enumerate((Wq, Wk, Wv)):
                sp.dma_start(wqkv[:, :, k * D:(k + 1) * D],
                             w.rearrange("(k p) n -> p k n", p=P)).then_inc(wqkv_in, 16)
            for k, b in enumerate((bq, bk, bv)):
                sp.dma_start(bqkv[:, k * D:(k + 1) * D],
                             b.rearrange("(a n) -> a n", a=1).partition_broadcast(P)).then_inc(wqkv_in, 16)

            sp.wait_ge(consts, 1)
            for l in lists:
                sp.dma_start(l.rearrange("(p c) k -> p (c k)", p=P), none[:, :]).then_inc(prefilled, 16)
            sp.dma_start(seen_t.rearrange("(p c) k -> p (c k)", p=HI), zeros[0:HI, :]).then_inc(prefilled, 16)

            def load_x(g, i, u, tail=False):
                if tail:
                    sp.dma_start(xg[0:REST, u, 0, :], x[P * T:N, :]).then_inc(ax_in[u], 16)
                else:
                    sp.dma_start(xg[:, u, :, :],
                                 grouped(x, D)[:, ds(g * G, G), :]).then_inc(ax_in[u], 16)

            def store_qkv(g, u, tail=False):
                if tail:
                    sp.dma_start(qkv_t[P * T:N, :], qkv[0:REST, u, 0, :]).then_inc(a_stored[u], 16)
                    sp.dma_start(attn_t[P * T:N, :], qkv[0:REST, u, 0, 2 * D:]).then_inc(a_stored[u], 16)
                else:
                    sp.dma_start(grouped(qkv_t, 3 * D)[:, ds(g * G, G), :], qkv[:, u, :, :])\
                      .then_inc(a_stored[u], 16)
                    sp.dma_start(grouped(attn_t, D)[:, ds(g * G, G), :], qkv[:, u, :, 2 * D:])\
                      .then_inc(a_stored[u], 16)

            def a_group(i, u, tail_next=False, load=True):
                g = 2 * i + u
                if load:
                    sp.wait_ge(a_h, g + 1)
                    load_x(g + 2, i, u, tail_next)
                sp.wait_ge(a_ev, 3 * g + 5)
                store_qkv(g, u)

            def a_loop(lo, hi):
                with sp.Fori(lo, hi) as i:
                    for u in range(2):
                        a_group(i, u)

            def load_list(k, p):
                sp.wait_ge(scattered, p)
                sp.dma_start(lst[:, :, :],
                             lists[k][LBASE:LBASE + JC * P, :].rearrange("(b j e) k -> j b (e k)", b=4, e=P))\
                  .then_inc(list_in, 16)

            load_x(0, 0, 0)
            load_x(1, 0, 1)
            sp.wait_ge(cnt_ready, 1)
            sp.dma_start(cnt_t.rearrange("(p c) k -> p (c k)", p=HI), cnt_s[:, :]).then_inc(cnt_stored, 16)
            a_loop(cuts[0], cuts[1])
            load_list(0, 1)
            a_loop(cuts[1], cuts[2])
            load_list(1, 2)
            a_loop(cuts[2], cuts[3])
            load_list(0, 3)
            a_loop(cuts[3], NGRP // 2 - 1)
            a_group(NGRP // 2 - 1, 0, tail_next=True)
            a_group(NGRP // 2 - 1, 1, load=False)
            sp.wait_ge(a_ev, 3 * NGRP + 3)
            store_qkv(NGRP, 0, tail=True)
            load_list(1, 4)
            for k, o in enumerate((-1, 1)):
                sp.dma_start(near[:, k, :, :],
                             lists[1][LBASE + o:LBASE + o + JC * P, :]
                             .rearrange("(b j e) k -> j b (e k)", b=4, e=P)).then_inc(list_in, 16)
            sp.wait_ge(reset_ready, 1)
            sp.dma_start(reset_t.rearrange("(b j) e -> j b e", b=4), reset_s[:, :, :])\
              .then_inc(reset_stored, 16)
            sp.wait_ge(reset_stored, 16)

            groups = sp.value_load(groups_i[0:1, 0:1], min_val=1, max_val=JC // 8)
            rows_of = lists[1].rearrange("(j e) k -> j (e k)", e=P)
            with sp.Fori(0, groups * 4) as i:
                for u in range(2):
                    sp.wait_ge(e_out[u], i + 1)
                    sp.dma_start(row_bc[:, u, :, :].rearrange("p e k -> p (e k)"),
                                 rows_of[ds(i * 2 + (u + 1), 1), :].partition_broadcast(P))\
                      .then_inc(e_row_in[u], 16)
                    sp.dma_start(reset_bc[:, u, :],
                                 reset_t[ds(i * 2 + u, 1), :].partition_broadcast(HEADS))\
                      .then_inc(e_row_in[u], 16)

            sp.wait_ge(e_end, 1)
            for k, (t, s) in enumerate(((cnt_t, cnt_n), (seen_t, seen_n))):
                sp.dma_start(s[:, 0:T], t[0:P * T, :].rearrange("(p t) c -> p (t c)", t=T))\
                  .then_inc(has_in, 16)
                sp.dma_start(s[0:REST, T:T + 1], t[P * T:N, :]).then_inc(has_in, 16)

            def load_b(g, u, tail=False):
                if tail:
                    sp.dma_start(xg[0:REST, u, 0, :], x[P * T:N, :]).then_inc(b_in[u], 16)
                    sp.dma_start(ag[0:REST, u, 0, :], attn_t[P * T:N, :]).then_inc(b_in[u], 16)
                else:
                    sp.dma_start(xg[:, u, :, :], grouped(x, D)[:, ds(g * G, G), :]).then_inc(b_in[u], 16)
                    sp.dma_start(ag[:, u, :, :], grouped(attn_t, D)[:, ds(g * G, G), :]).then_inc(b_in[u], 16)

            def b_group(i, u, load=True, tail_next=False):
                g = 2 * i + u
                if load:
                    sp.wait_ge(b_xb, g + 1)
                    sp.wait_ge(b_tp, 3 * g + 3)
                    load_b(g + 2, u, tail_next)
                sp.wait_ge(b_u, g + 3)
                sp.dma_start(grouped(out, D)[:, ds(g * G, G), :], ug[:, u, :, :]).then_inc(b_stored[u], 16)

            load_b(0, 0)
            load_b(1, 1)
            with sp.Fori(0, NGRP // 2 - 1) as i:
                for u in range(2):
                    b_group(i, u)
            b_group(NGRP // 2 - 1, 0, tail_next=True)
            b_group(NGRP // 2 - 1, 1, load=False)
            sp.wait_ge(b_u, NGRP + 3)
            sp.dma_start(out[P * T:N, :], ug[0:REST, 0, 0, :]).then_inc(b_stored[0], 16)

            sp.wait_ge(norm_ready, 1)
            sp.dma_start(grouped(norm_t, 4), norm_s[:, 0:T, :]).then_inc(norm_stored, 16)
            sp.dma_start(norm_t[P * T:N, :], norm_s[0:REST, T, :]).then_inc(norm_stored, 16)

        @block.gpsimd
        def _(pool):
            for k, s in enumerate((*sum(scat, []), *e_sc, *f_sc)):
                pool.dma_start(opened[:, 4 + k, :], x[0:16, 0:16]).then_inc(s, 16)
            table_end = pool.to_reg(N - 1)
            list_end = pool.to_reg(LLEN - 1)

            def alone():
                pool.sem_inc(aside, 1)

            pool.iota(iota[:, :], [[1, LO]], base=0, channel_multiplier=0).then_inc(iota_ready, 1)
            pool.memset(ones_b[:, :], 1.0)
            pool.memset(zeros_b[:, :], 0.0)
            pool.memset(zeros[:, :], 0.0)
            pool.memset(ones[:, :], 1.0)
            pool.memset(eps[:, :], EPS)
            pool.memset(none[:, :], NONE)
            pool.memset(ident[:, :], 0.0)
            pool.memset(from_here[:, :], -1.0)
            pool.memset(before[:, :], 1.0)
            pool.iota(digits[:, :], [[1, 16]], base=0, channel_multiplier=0,
                      allow_small_or_imprecise_dtypes=True)
            for k in range(16):
                pool.memset(bits[:, k:k + 1], float(1 << (15 - k)))
            pool.iota(node[:, 0:T], [[1, T]], base=0, channel_multiplier=T)
            pool.iota(node[:, T:TC], [[0, G]], base=P * T, channel_multiplier=1)
            pool.drain()
            pool.affine_select(out=ident[:, :], in_=ident[:, :], compare_op=ALU.not_equal, fill=1.0,
                               base=0, pattern=[[-1, P]], channel_multiplier=1)
            pool.affine_select(out=from_here[:, :], in_=from_here[:, :], compare_op=ALU.is_ge, fill=0.0,
                               base=0, pattern=[[-1, P]], channel_multiplier=1)
            pool.affine_select(out=before[:, :], in_=before[:, :], compare_op=ALU.is_gt, fill=0.0,
                               base=0, pattern=[[1, P]], channel_multiplier=-1)
            for t in (ends, rows_in, cntg, fn, cnt_n, seen_n):
                pool.memset(t[:], 0.0)
            pool.iota(pcol[:, :], [[0, 1]], base=0, channel_multiplier=1,
                      allow_small_or_imprecise_dtypes=True)
            pool.affine_select(out=live[:, :], in_=ones[:, 0:1], compare_op=ALU.is_gt, fill=0.0,
                               base=REST, pattern=[[0, 1]], channel_multiplier=-1)
            pool.drain().then_inc(consts, 1)

            pool.wait_ge(prefilled, 48)
            pool.wait_ge(pos_ready, 1)

            def scatter_block(k, u, start, width, n, count, target):
                pool.wait_ge(scat[k][u], count + 16)
                pool.tensor_copy(idx_blk[0:n, u, 0:width], pos_i[0:n, ds(start, width)])
                pool.tensor_copy(pay_blk[0:n, u, 0:width, :], pay[0:n, ds(start, width), :])
                pool.drain()
                for c in range(width):
                    pool.indirect_dma_start(target, IDX(ap=idx_blk[0:n, u, c:c + 1], axis=0),
                                            pay_blk[0:n, u, c, :], None,
                                            bounds_check=list_end, oob_is_err=False)\
                        .then_inc(scat[k][u], 16)

            with pool.Fori(0, EC // 20) as i:
                for u in range(2):
                    scatter_block(0, u, i * 20 + u * 10, 10, EP, i * 160, lists[0])
            for u in range(2):
                pool.wait_ge(scat[0][u], EC // 20 * 160 + 16)
            pool.sem_inc(scattered, 1)

            pool.wait_ge(groups_ready, 1)
            groups = pool.value_load(groups_i[0:1, 0:1], min_val=1, max_val=JC // 8)
            for k in range(1, 4):
                pool.wait_ge(pos_ready, k + 1)
                with pool.Fori(0, groups) as i:
                    for u in range(2):
                        scatter_block(k, u, i * 8 + u * 4, 4, P, i * 64, lists[k % 2])
                for u in range(2):
                    pool.wait_ge(scat[k][u], groups * 64 + 16)
                pool.sem_inc(scattered, 1)

            def gather(j, u):
                pool.tensor_copy(gidx[:, u, :], idx_all[:, ds(j, 1), :].rearrange("p a k -> p (a k)"))
                pool.drain()
                for t, k, dest in ((qkv_t, 0, rowg[:, u, :]), (qkv_t, 1, colg[:, u, :]),
                                   (cnt_t, 0, cntg[:, u, :])):
                    pool.indirect_dma_start(dest, None, t, IDX(ap=gidx[:, u, k:k + 1], axis=0),
                                            bounds_check=table_end, oob_is_err=False)\
                        .then_inc(e_in[u], 16)

            pool.wait_ge(cols_ready, 1)
            pool.wait_ge(cnt_stored, 16)
            for u in range(2):
                pool.wait_ge(a_stored[u], 32 * (NGRP // 2 + (u == 0)) + 16)
                alone()
                gather(u, u)
            with pool.Fori(0, groups * 4) as i:
                for u in range(2):
                    pool.wait_ge(e_out[u], i + 2)
                    pool.wait_ge(e_sc[u], i * 32 + 16)
                    alone()
                    pool.tensor_copy(sidx[:, u, :], idx_all[:, ds(i * 2 + u, 1), 2])
                    pool.drain()
                    for t, s in ((attn_t, outb[:, u, :]), (seen_t, ones[:, 0:1])):
                        pool.indirect_dma_start(t, IDX(ap=sidx[:, u, :], axis=0), s, None,
                                                bounds_check=table_end, oob_is_err=False)\
                            .then_inc(e_sc[u], 16)
                    gather(i * 2 + (u + 2), u)
            for u in range(2):
                pool.wait_ge(e_sc[u], groups * 128 + 16)
                pool.wait_ge(e_in[u], groups * 192 + 48)
            pool.sem_inc(e_end, 1)

            def b_group(i, u):
                g = 2 * i + u
                pool.wait_ge(b_in[u], 32 * i + 32)
                pool.wait_ge(b_x1, g + 1)
                pool.tensor_tensor(xb[:, u, :, :], xg[:, u, :, :],
                                   bos[:, :].unsqueeze(1).to_broadcast([P, G, D]), ALU.add)\
                    .then_inc(b_xb, 1)

            pool.wait_ge(late_in, 16 * 8)
            with pool.Fori(0, NGRP // 2) as i:
                for u in range(2):
                    b_group(i, u)
            b_group(NGRP // 2, 0)

            def f_gather(g, i, u):
                pool.wait_ge(f_sc[u], i * (FG * 16) + 16)
                alone()
                pool.tensor_copy(fidx[:, u, :], chosen[:, ds(g * FG, FG)])
                pool.drain()
                for c in range(FG):
                    for t, dest in ((out, fu[:, u, c, :]), (norm_t, fn[:, u, c, :])):
                        pool.indirect_dma_start(dest, None, t, IDX(ap=fidx[:, u, c:c + 1], axis=0),
                                                bounds_check=table_end, oob_is_err=False)\
                            .then_inc(f_in[u], 16)

            def f_scatter(g, u):
                pool.wait_ge(f_o, g + 1)
                alone()
                for c in range(FG):
                    pool.indirect_dma_start(out, IDX(ap=fidx[:, u, c:c + 1], axis=0),
                                            fo[:, u, c, :], None,
                                            bounds_check=table_end, oob_is_err=False)\
                        .then_inc(f_sc[u], 16)

            pool.wait_ge(ch_ready, 1)
            pool.wait_ge(norm_stored, 32)
            for u in range(2):
                pool.wait_ge(b_stored[u], 16 * (NGRP // 2 + (u == 0)) + 16)
            f_gather(0, 0, 0)
            with pool.Fori(0, (NFG - 1) // 2) as i:
                f_gather(i * 2 + 1, i, 1)
                f_scatter(i * 2, 0)
                f_gather(i * 2 + 2, i + 1, 0)
                f_scatter(i * 2 + 1, 1)
            r = (NFG - 1) // 2
            if NFG % 2 == 0:
                f_gather(NFG - 1, r, 1)
            f_scatter(2 * r, 0)
            if NFG % 2 == 0:
                f_scatter(NFG - 1, 1)
            for u in range(2):
                pool.wait_ge(f_sc[u], FG * 16 * ((NFG + 1 - u) // 2) + 16)

        @block.scalar
        def _(act):
            act.dma_start(wo[:, :, :], Wo.rearrange("(k p) n -> p k n", p=P)).then_inc(late_in, 16)
            act.dma_start(w1s[:, :, :], w1.rearrange("(k p) n -> p k n", p=P)).then_inc(late_in, 16)
            act.dma_start(w2s[:, :, :], w2.rearrange("(k p) n -> p k n", p=P)).then_inc(late_in, 16)
            act.dma_start(b1s[:, :], b1.rearrange("(k p) -> p k", p=P),
                          allow_slow_non_contiguous=True).then_inc(late_in, 16)
            act.dma_start(brs[:, :], br.rearrange("(a n) -> a n", a=1).partition_broadcast(P))\
                .then_inc(late_in, 16)
            for s, v in ((bos, bo), (b2s, b2)):
                act.dma_start(s[:, :], v.rearrange("(a n) -> a n", a=1).partition_broadcast(P))\
                    .then_inc(late_in, 16)
            act.dma_start(wrs[:, :], wr.rearrange("n a -> a n").partition_broadcast(P))\
                .then_inc(late_in, 16)
            for s in (a_ht, b_at, f_zt, f_h, b_u):
                act.sem_inc(s, 2)
            act.wait_ge(consts, 1)

            def a_group(i, u):
                g = 2 * i + u
                for k in range(G):
                    if k == 1:
                        a_dev(g + 1, 1 - u)
                    act.wait_ge(a_tp, 3 * g + k + 1)
                    act.activation(ht[:, u, k, :], tp_ps[(u * G + k) % 2][:, 0:D], ACT.Copy)\
                        .then_inc(a_ht, 1)

            def a_dev(g, u):
                act.wait_ge(a_var, g + 1)
                act.activation(sd[:, u, :], mv[:, u, :, 1], ACT.Sqrt, bias=eps[:, 0:1]).then_inc(a_sd, 1)

            a_dev(0, 0)
            with act.Fori(0, NGRP // 2) as i:
                for u in range(2):
                    a_group(i, u)
            for k in range(G):
                act.wait_ge(a_tp, 3 * NGRP + k + 1)
                act.activation(ht[:, 0, k, :], tp_ps[k % 2][:, 0:D], ACT.Copy).then_inc(a_ht, 1)

            act.wait_ge(groups_ready, 1)
            groups = act.value_load(groups_i[0:1, 0:1], min_val=1, max_val=JC // 8)
            with act.Fori(0, groups * 4) as i:
                for u in range(2):
                    c = i * 2 + u
                    act.wait_ge(e_rt, c + 1)
                    act.activation(runt[:, :], half[1][:, 0:HEADS], ACT.Copy).then_inc(e_runt, 1)
                    act.wait_ge(e_max, c + 1)
                    act.activation(state[:, u, 0:HEADS], half[2][:, 0:HEADS], ACT.Copy)\
                        .then_inc(e_cmax, 1)
                    act.wait_ge(e_expo, c + 1)
                    act.activation(ex[:, :, :], expo[:, :, :], ACT.Exp).then_inc(e_ex, 1)

            def b_dev(g, u):
                act.wait_ge(b_var, g + 1)
                act.activation(sd[:, u, :], mv[:, u, :, 1], ACT.Sqrt, bias=eps[:, 0:1]).then_inc(b_sd, 1)

            def b_ht(g, u):
                for k in range(G):
                    act.wait_ge(b_tp, 3 * g + k + 1)
                    act.activation(ht[:, u, k, :], tp_ps[(u * G + k) % 2][:, 0:D], ACT.Copy)\
                        .then_inc(b_at, 1)

            def b_sum(i, u):
                g = 2 * i + u
                act.wait_ge(b_gain, g + 1)
                act.wait_ge(b_stored[u], 16 * i + 16)
                for k in range(G):
                    last = act.activation(ug[:, u, k, :], x1[:, u, k, :], ACT.Identity,
                                          bias=shift[:, u, k:k + 1], scale=gain[:, u, k:k + 1])
                last.then_inc(b_u, 1)

            b_ht(0, 0)
            b_dev(0, 0)
            with act.Fori(0, NGRP // 2) as i:
                for u in range(2):
                    g = i * 2 + u
                    b_ht(g + 1, 1 - u)
                    b_dev(g + 1, 1 - u)
                    b_sum(i, u)
            b_sum(NGRP // 2, 0)

            def f_trans(g, u):
                for c in range(FG):
                    act.wait_ge(f_tp, FG * g + c + 1)
                    act.activation(fzt[:, u, :, c * P:(c + 1) * P],
                                   tp_ps[c % 2][:, 0:D].rearrange("p (k n) -> p k n", k=KT), ACT.Copy)\
                        .then_inc(f_zt, 1)

            def f_gelu(g, u):
                for k in range(HT):
                    act.wait_ge(f_m1, HT * g + k + 1)
                    act.activation(fh[:, u, k, :], half[k % 2], ACT.Gelu_apprx_tanh,
                                   bias=b1s[:, k:k + 1]).then_inc(f_h, 1)

            f_trans(0, 0)
            r = (NFG - 1) // 2
            with act.Fori(0, r) as i:
                for u in range(2):
                    f_gelu(i * 2 + u, u)
                    f_trans(i * 2 + (u + 1), 1 - u)
            f_gelu(2 * r, 0)
            if NFG % 2 == 0:
                f_trans(NFG - 1, 1)
                f_gelu(NFG - 1, 1)

        @block.tensor
        def _(pe):
            pe.wait_ge(consts, 1)
            hist = sort_ps[0][:, 0:LO]
            pe.sem_inc(hist_free, 4)
            pe.sem_inc(ch_free, 4)
            pe.matmul(hist, zeros_b[0:EP, 0:P], zeros_b[0:EP, :], start=True, stop=False)
            with pe.Fori(0, EC // 4) as i:
                for k in range(4):
                    pe.wait_ge(hist_oh, i * 4 + k + 1)
                    pe.matmul(hist, oh_hi[:, k, :], oh_lo[:, k, :], start=False, stop=False)\
                        .then_inc(hist_free, 1)
            pe.matmul(hist, zeros_b[0:EP, 0:P], zeros_b[0:EP, :], start=False, stop=True)\
                .then_inc(hist_done, 1)

            def rank_pass(k, n, w):
                with pe.Fori(0, 16) as d:
                    pe.wait_ge(sort_oh, d + (16 * k + 1))
                    pe.matmul(sort_ps[0][0:n, 0:w], from_here[0:n, 0:n], onehot[0:n, 0:w],
                              start=True, stop=True)
                    pe.matmul(sort_ps[1][0:n, 0:w], ones_b[0:n, 0:n], onehot[0:n, 0:w],
                              start=True, stop=True).then_inc(sort_mm, 1)

            def turn_list(k, parts):
                pe.wait_ge(list_f, k)
                for s, dest in parts:
                    for b in range(4):
                        last = pe.transpose(dest[:, b * JB:(b + 1) * JB], s[:, b, :], ident[0:JB, 0:JB])
                last.then_inc(list_t, 1)

            def a_trans(g, u, k):
                n = u * G + k
                if k == 0:
                    pe.wait_ge(a_h, g + 1)
                pe.wait_ge(a_ht, 3 * g + k + 1)
                for c in range(KT):
                    last = pe.transpose(tp_ps[n % 2][:, c * P:(c + 1) * P],
                                        h[:, u, k, c * P:(c + 1) * P], ident[:, :])
                last.then_inc(a_tp, 1)

            def a_proj(g, u, k):
                pe.wait_ge(a_ht, 3 * g + k + 3)
                pe.wait_ge(a_ev, 3 * g + k + 1)
                ps = qkv_ps[(u * G + k) % 2]
                for a, b in ((0, 2 * D), (2 * D, 3 * D)):
                    for c in range(KT):
                        last = pe.matmul(ps[:, a:b], ht[:, u, k, c * P:(c + 1) * P], wqkv[:, c, a:b],
                                         start=(c == 0), stop=(c == KT - 1))
                last.then_inc(a_mm, 1)

            def a_group(i, u):
                g = 2 * i + u
                for k in range(G):
                    a_proj(g, u, k)
                    a_trans(g + 1, 1 - u, k)

            def a_loop(lo, hi):
                with pe.Fori(lo, hi) as i:
                    for u in range(2):
                        a_group(i, u)

            pe.wait_ge(wqkv_in, 96)
            rank_pass(0, EP, EC)
            for k in range(G):
                a_trans(0, 0, k)
            a_loop(cuts[0], cuts[1])
            for p, (lo, hi) in enumerate(((cuts[1], cuts[2]), (cuts[2], cuts[3]), (cuts[3], NGRP // 2))):
                turn_list(p + 1, ((lst_f[:, 0], sort_ps[0]), (lst_f[:, 1], sort_ps[1])))
                rank_pass(p + 1, P, JC)
                a_loop(lo, hi)
            for k in range(G):
                a_proj(NGRP, 0, k)
            turn_list(4, ((lst_f[:, 0], sort_ps[0]), (lst_f[:, 1], sort_ps[1]),
                          (near_f[:, 0], tp_ps[0]), (near_f[:, 1], tp_ps[1])))

            pe.wait_ge(groups_ready, 1)
            groups = pe.value_load(groups_i[0:1, 0:1], min_val=1, max_val=JC // 8)
            pe.wait_ge(cols_ready, 1)
            with pe.Fori(0, groups * 4) as i:
                for u in range(2):
                    c = i * 2 + u
                    pe.wait_ge(e_smax, c + 1)
                    pe.transpose(half[0][0:HEADS, 0:P], smax[:, :], ident[:, :]).then_inc(e_st, 1)
                    pe.wait_ge(e_state, c + 1)
                    pe.matmul(half[3][:, 0:2 * HEADS + D], carrym[:, :], state[:, 1 - u, :],
                              start=True, stop=True)
                    pe.wait_ge(e_run, c + 1)
                    pe.sem_inc(aside, 1)
                    pe.transpose(half[1][:, 0:HEADS], run[:, u, :], ident[0:HEADS, 0:HEADS])\
                        .then_inc(e_rt, 1)
                    pe.wait_ge(e_runt, c + 1)
                    pe.matmul(half[2][:, 0:HEADS], lastm[:, :], runt[:, :], start=True, stop=True)\
                        .then_inc(e_max, 1)
                    pe.wait_ge(e_pv, c + 1)
                    pe.matmul(tp_ps[0][:, 0:D + HEADS], same[:, :], pv[:, :], start=True, stop=True)\
                        .then_inc(e_sum, 1)

            def b_trans(g, i, u):
                pe.wait_ge(b_in[u], 32 * i + 32)
                for k in range(G):
                    pe.wait_ge(b_at, 3 * g + k + 1)
                    for c in range(KT):
                        last = pe.transpose(tp_ps[(u * G + k) % 2][:, c * P:(c + 1) * P],
                                            ag[:, u, k, c * P:(c + 1) * P], ident[:, :])
                    last.then_inc(b_tp, 1)

            def b_proj(g, u):
                for k in range(G):
                    pe.wait_ge(b_at, 3 * g + k + 3)
                    pe.wait_ge(b_x1t, 3 * g + k + 1)
                    ps = half[(u * G + k) % 2 * 2]
                    for c in range(KT):
                        last = pe.matmul(ps[:, 0:D], ht[:, u, k, c * P:(c + 1) * P], wo[:, c, :],
                                         start=(c == 0), stop=(c == KT - 1))
                    last.then_inc(b_mm, 1)

            pe.wait_ge(late_in, 128)
            b_trans(0, 0, 0)
            b_proj(0, 0)
            with pe.Fori(0, NGRP // 2) as i:
                b_trans(i * 2 + 1, i, 1)
                b_proj(i * 2 + 1, 1)
                b_trans(i * 2 + 2, i + 1, 0)
                b_proj(i * 2 + 2, 0)

            with pe.Fori(0, 32) as s:
                pe.wait_ge(t_cnt, s + 1)
                pe.matmul(half[1][:, 0:1], ones[:, :], cntc[:, :], start=True, stop=True)\
                    .then_inc(t_sum, 1)
            for s, m in ((32, ones), (33, before), (34, before), (35, ones), (36, before)):
                pe.wait_ge(t_cnt, s + 1)
                pe.matmul(half[1][:, 0:1], m[:, :], cntc[:, :], start=True, stop=True)\
                    .then_inc(t_sum, 1)

            def list_column(k, wait, **flags):
                pe.wait_ge(ch_oh, wait)
                for s in range(2):
                    last = pe.matmul(sort_ps[s][:, 0:FC], oh_slot[:, k, s, :], oh_col[:, k, :], **flags)
                last.then_inc(ch_free, 1)

            for s in range(2):
                pe.matmul(sort_ps[s][:, 0:FC], zeros_b[:, 0:P], zeros_b[:, 0:FC], start=True, stop=False)
            with pe.Fori(0, T // 4) as i:
                for k in range(4):
                    list_column(k, i * 4 + k + 1, start=False, stop=False)
            for k in range(T // 4 * 4, T):
                list_column(k % 4, k + 1, start=False, stop=False)
            list_column(T % 4, T + 1, start=False, stop=True)
            pe.drain().then_inc(ch_done, 1)

            def f_trans(g, u):
                pe.wait_ge(f_z, g + 1)
                for c in range(FG):
                    pe.wait_ge(f_zt, FG * g + c + 1)
                    for k in range(KT):
                        last = pe.transpose(tp_ps[c % 2][:, k * P:(k + 1) * P],
                                            fz[:, u, c, k * P:(k + 1) * P], ident[:, :])
                    last.then_inc(f_tp, 1)

            def f_up(g, u):
                pe.wait_ge(f_zt, FG * g + FG + 2)
                for k in range(HT):
                    pe.wait_ge(f_h, HT * g + k + 1)
                    for c in range(KT):
                        last = pe.matmul(half[k % 2], w1s[:, c, k * P:(k + 1) * P], fzt[:, u, c, :],
                                         start=(c == 0), stop=(c == KT - 1))
                    last.then_inc(f_m1, 1)

            def f_down(g, u):
                pe.wait_ge(f_h, HT * g + HT + 2)
                for c in range(FG):
                    pe.wait_ge(f_y, FG * g + c + 1)
                    for k in range(HT):
                        last = pe.matmul(half[2 + c % 2][:, 0:D], fh[:, u, k, c * P:(c + 1) * P],
                                         w2s[:, k, :], start=(k == 0), stop=(k == HT - 1))
                    last.then_inc(f_m2, 1)

            f_trans(0, 0)
            r = (NFG - 1) // 2
            with pe.Fori(0, r) as i:
                for u in range(2):
                    f_up(i * 2 + u, u)
                    f_trans(i * 2 + (u + 1), 1 - u)
                    f_down(i * 2 + u, u)
            f_up(2 * r, 0)
            if NFG % 2 == 0:
                f_trans(NFG - 1, 1)
            f_down(2 * r, 0)
            if NFG % 2 == 0:
                f_up(NFG - 1, 1)
                f_down(NFG - 1, 1)

        @block.vector
        def _(dve):
            for s in (a_ev, b_x1, b_x1t, f_y):
                dve.sem_inc(s, 2)
            for s in e_out:
                dve.sem_inc(s, 1)
            dve.memset(state[:], 0.0)
            dve.memset(run[:], -BIG)
            dve.memset(idx_all[:], NONE)
            dve.memset(col_carry[:], -1.0)
            dve.drain().then_inc(e_state, 1)

            dve.wait_ge(edges_in, 32)
            dve.tensor_copy(edge_f[:, :, :], edge[:, :, :])
            dve.tensor_scalar(lo_i[:, :], edge[:, 0, :], LO - 1, None, ALU.bitwise_and)
            dve.tensor_scalar(hi_i[:, :], edge[:, 0, :], LO.bit_length() - 1, None, ALU.logical_shift_right)
            for k in range(2):
                dve.tensor_copy(pay[0:EP, 0:EC, k], edge[:, k, :])
            dve.drain()
            dve.tensor_tensor(is_self[:, :], edge_f[:, 0, :], edge_f[:, 1, :], ALU.is_equal)
            dve.tensor_copy(lo_f[:, :], lo_i[:, :])
            dve.tensor_copy(hi_f[:, :], hi_i[:, :])
            dve.drain()
            dve.scalar_tensor_tensor(lo_f[:, :], lo_f[:, :], 1.0, is_self[:, :], ALU.add, ALU.mult)
            dve.drain()
            dve.tensor_scalar(lo_f[:, :], lo_f[:, :], -1.0, None, ALU.add)
            dve.drain()
            dve.wait_ge(iota_ready, 1)
            with dve.Fori(0, EC // 4) as i:
                for k in range(4):
                    dve.wait_ge(hist_free, i * 4 + k + 1)
                    dve.tensor_scalar(oh_hi[:, k, :], iota[0:EP, 0:P], hi_f[:, ds(i * 4 + k, 1)], None,
                                      ALU.is_equal)
                    dve.tensor_scalar(oh_lo[:, k, :], iota[0:EP, :], lo_f[:, ds(i * 4 + k, 1)], None,
                                      ALU.is_equal).then_inc(hist_oh, 1)
            dve.wait_ge(hist_done, 1)
            dve.tensor_copy(cnt_s[:, :], sort_ps[0][0:HI, 0:LO]).then_inc(cnt_ready, 1)

            def rank_pass(k, n, w):
                dve.memset(base[:, :], float(LBASE))
                dve.memset(pos[0:n, 0:w], FAR)
                dve.drain()
                with dve.Fori(0, 16) as d:
                    dve.tensor_scalar(onehot[0:n, 0:w], digit[0:n, 0:w], digits[0:n, ds(d, 1)], None,
                                      ALU.is_equal).then_inc(sort_oh, 1)
                    dve.wait_ge(sort_mm, d + (16 * k + 1))
                    dve.tensor_tensor_scan(upto[0:n, 0:w], sort_ps[1][0:n, 0:w], zeros[0:n, 0:w],
                                           base[0:n, 0:1], ALU.add, ALU.add)
                    dve.drain()
                    dve.tensor_tensor(place[0:n, 0:w], upto[0:n, 0:w], sort_ps[0][0:n, 0:w], ALU.add)
                    dve.tensor_copy(base[0:n, :], upto[0:n, w - 1:w])
                    dve.drain()
                    dve.copy_predicated(pos[0:n, 0:w], onehot[0:n, 0:w].bitcast(u16), place[0:n, 0:w])
                    dve.drain()
                dve.tensor_copy(pos_i[0:n, 0:w], pos[0:n, 0:w]).then_inc(pos_ready, 1)

            def list_floats(k):
                dve.wait_ge(list_in, 16 * k + (32 if k == 4 else 0))
                for s in range(2):
                    dve.tensor_copy(lst_f[:, s, :, :],
                                    lst[:, :, :].rearrange("j b (e k) -> j b e k", k=2)[:, :, :, s])
                    if k == 4:
                        dve.tensor_copy(near_f[:, s, :, :],
                                        near[:, s, :, :].rearrange("j b (e k) -> j b e k", k=2)[:, :, :, 0])
                dve.drain().then_inc(list_f, 1)
                dve.wait_ge(list_t, k)

            def list_pass(k):
                list_floats(k)
                dve.tensor_copy(row_i[:, :], sort_ps[0][:, 0:JC])
                dve.tensor_copy(pay[:, 0:JC, 0], sort_ps[0][:, 0:JC])
                dve.tensor_copy(pay[:, 0:JC, 1], sort_ps[1][:, 0:JC])
                dve.drain()
                dve.tensor_scalar(digit_i[:, 0:JC], row_i[:, :], 4 * k, 15, ALU.logical_shift_right,
                                  ALU.bitwise_and)
                dve.drain()
                dve.tensor_copy(digit[:, 0:JC], digit_i[:, 0:JC])
                dve.drain()
                rank_pass(k, P, JC)

            dve.tensor_scalar(digit_i[0:EP, 0:EC], edge[:, 0, :], 15, None, ALU.bitwise_and)
            dve.drain()
            dve.scalar_tensor_tensor(digit[0:EP, 0:EC], is_self[:, :], 16.0, digit_i[0:EP, 0:EC],
                                     ALU.mult, ALU.add)
            dve.drain()
            rank_pass(0, EP, EC)
            dve.tensor_scalar(groups_f[0:1, :], base[0:1, :], -float(LBASE), 1.0, ALU.add, ALU.max)
            dve.drain()
            dve.tensor_scalar(groups_i[0:1, :], groups_f[0:1, :], 8.0 * P - 1, None, ALU.add)
            dve.drain()
            dve.tensor_scalar(groups_i[0:1, :], groups_i[0:1, :], (8 * P).bit_length() - 1, None,
                              ALU.logical_shift_right).then_inc(groups_ready, 1)

            def a_stats(g, i, u):
                dve.wait_ge(ax_in[u], 16 * i + 16)
                for k in range(G):
                    dve.bn_stats(stats[:, u, k, :], xg[:, u, k, :])
                dve.drain()
                for k in range(G):
                    last = dve.bn_aggr(mv[:, u, k, :], stats[:, u, k, :])
                last.then_inc(a_var, 1)

            def a_norm(g, u):
                dve.wait_ge(a_sd, g + 1)
                dve.reciprocal(rs[:, u, :], sd[:, u, :])
                dve.drain()
                for k in range(G):
                    last = dve.tensor_scalar(h[:, u, k, :], xg[:, u, k, :], mv[:, u, k, 0:1],
                                             rs[:, u, k:k + 1], ALU.subtract, ALU.mult)
                last.then_inc(a_h, 1)

            def a_evac(g, u, k):
                dve.wait_ge(a_mm, 3 * g + k + 1)
                dve.tensor_tensor(qkv[:, u, k, :], qkv_ps[(u * G + k) % 2][:, 0:3 * D], bqkv[:, :], ALU.add)\
                    .then_inc(a_ev, 1)

            def a_group(i, u, ahead=True):
                g = 2 * i + u
                a_norm(g + 1, 1 - u)
                dve.wait_ge(a_stored[u], 32 * i + 16)
                a_evac(g, u, 0)
                if ahead:
                    a_stats(g + 2, i + 1, u)
                a_evac(g, u, 1)
                a_evac(g, u, 2)

            def a_loop(lo, hi):
                with dve.Fori(lo, hi) as i:
                    for u in range(2):
                        a_group(i, u)

            dve.wait_ge(wqkv_in, 96)
            dve.wait_ge(consts, 1)
            a_stats(0, 0, 0)
            a_norm(0, 0)
            a_stats(1, 0, 1)
            a_loop(cuts[0], cuts[1])
            list_pass(1)
            a_loop(cuts[1], cuts[2])
            list_pass(2)
            a_loop(cuts[2], cuts[3])
            list_pass(3)
            a_loop(cuts[3], NGRP // 2 - 1)
            a_group(NGRP // 2 - 1, 0)
            a_group(NGRP // 2 - 1, 1, ahead=False)
            dve.wait_ge(a_stored[0], 32 * (NGRP // 2) + 16)
            for k in range(G):
                a_evac(NGRP, 0, k)

            list_floats(4)
            row_ps, col_ps, prev_ps, next_ps = [b[:, 0:JC] for b in (*sort_ps, *tp_ps)]
            dve.tensor_copy(col_row[:, 0:JC], row_ps)
            dve.tensor_copy(col_next[:, 0:JC], next_ps)
            dve.tensor_copy(idx_all[:, 0:JC, 0], row_ps)
            dve.tensor_copy(idx_all[:, 0:JC, 1], col_ps)
            dve.tensor_tensor(reset_s[:, :, :], lst_f[:, 0, :, :], near_f[:, 0, :, :], ALU.not_equal)
            dve.drain()
            dve.tensor_scalar(reset_s[:, :, :], reset_s[:, :, :], -BIG, None, ALU.mult).then_inc(reset_ready, 1)
            dve.tensor_tensor(col_last[:, 0:JC], col_row[:, 0:JC], col_next[:, 0:JC], ALU.not_equal)
            dve.tensor_tensor(col_next[:, 0:JC], col_row[:, 0:JC], col_next[:, 0:JC], ALU.is_equal)
            dve.drain()
            dve.scalar_tensor_tensor(col_next[:, 0:JC], col_next[:, 0:JC], FAR, col_row[:, 0:JC],
                                     ALU.mult, ALU.add)
            dve.tensor_scalar(col_last[:, 0:JC], col_last[:, 0:JC], ident[:, P - 1:P], None, ALU.max)
            dve.tensor_scalar(col_carry[:, 1:JC + 1], col_row[:, 0:JC], 1.0, ident[:, P - 1:P],
                              ALU.add, ALU.mult)
            dve.drain()
            dve.tensor_copy(idx_all[:, 0:JC, 2], col_next[:, 0:JC])
            dve.tensor_scalar(col_carry[:, 1:JC + 1], col_carry[:, 1:JC + 1], -1.0, None, ALU.add)
            dve.drain().then_inc(cols_ready, 1)

            groups = dve.value_load(groups_i[0:1, 0:1], min_val=1, max_val=JC // 8)

            def heads(t):
                return t.rearrange("p (h d) -> p h d", h=HEADS)

            def over_heads(t):
                return t.unsqueeze(2).to_broadcast([P, HEADS, HD])

            with dve.Fori(0, groups * 4) as i:
                for u in range(2):
                    c = i * 2 + u
                    dve.wait_ge(e_row_in[u], 32 * i + 32)
                    dve.wait_ge(e_in[u], 48 * i + 48)
                    q, k_row, v_row = (rowg[:, u, s * D:(s + 1) * D] for s in range(3))
                    k_col, v_col = (colg[:, u, s * D:(s + 1) * D] for s in range(1, 3))
                    row = col_row[:, ds(c, 1)]
                    dve.tensor_tensor(qk[:, 0, :], q, k_col, ALU.mult)
                    dve.tensor_tensor(qk[:, 1, :], q, k_row, ALU.mult)
                    dve.tensor_scalar(same[:, :], row_bc[:, u, :, 0], row, None, ALU.is_equal)
                    dve.tensor_scalar(lastm[:, :], row_bc[:, u, :, 0], row, col_last[:, ds(c, 1)],
                                      ALU.is_equal, ALU.mult)
                    dve.tensor_scalar(carrym[:, :], row_bc[:, u, :, 0], col_carry[:, ds(c, 1)], None,
                                      ALU.is_equal)
                    dve.tensor_scalar(no_self[:, :], cntg[:, u, :], 0.0, -BIG, ALU.is_equal, ALU.mult)
                    dve.drain()
                    dve.tensor_reduce(raw[:, :, :], qk[:, :, :].rearrange("p s (h d) -> p s h d", h=HEADS),
                                      AX, ALU.add)
                    dve.drain()
                    dve.tensor_scalar(sc[:, 0, :], raw[:, 0, :], SCALE, None, ALU.mult)
                    dve.tensor_scalar(sc[:, 1, :], raw[:, 1, :], SCALE, no_self[:, :], ALU.mult, ALU.add)
                    dve.drain()
                    dve.tensor_tensor(smax[:, :], sc[:, 0, :], sc[:, 1, :], ALU.max).then_inc(e_smax, 1)
                    dve.wait_ge(e_st, c + 1)
                    dve.tensor_tensor_scan(run[:, u, :], reset_bc[:, u, :], half[0][0:HEADS, 0:P],
                                           run[:, 1 - u, P - 1:P], ALU.add, ALU.max).then_inc(e_run, 1)
                    dve.wait_ge(e_cmax, c + 1)
                    top = state[:, u, 0:HEADS]
                    dve.tensor_tensor(expo[:, 0, :], sc[:, 0, :], top, ALU.subtract)
                    dve.tensor_tensor(expo[:, 1, :], sc[:, 1, :], top, ALU.subtract)
                    dve.tensor_tensor(expo[:, 2, :], half[3][:, 0:HEADS], top, ALU.subtract)
                    dve.drain()
                    dve.tensor_scalar(expo[:, :, :], expo[:, :, :], 0.0, None, ALU.min).then_inc(e_expo, 1)
                    dve.wait_ge(e_ex, c + 1)
                    dve.tensor_tensor(heads(pv[:, 0:D]), heads(v_col), over_heads(ex[:, 0, :]), ALU.mult)
                    dve.tensor_copy(pv[:, D:D + HEADS], ex[:, 0, :]).then_inc(e_pv, 1)
                    dve.tensor_scalar(selfw[:, :], ex[:, 1, :], cntg[:, u, :], None, ALU.mult)
                    dve.tensor_tensor(heads(carried[:, 0:D]), heads(half[3][:, HEADS:HEADS + D]),
                                      over_heads(ex[:, 2, :]), ALU.mult)
                    dve.tensor_tensor(carried[:, D:], half[3][:, HEADS + D:2 * HEADS + D], ex[:, 2, :],
                                      ALU.mult)
                    dve.drain()
                    dve.tensor_tensor(heads(selfv[:, :]), heads(v_row), over_heads(selfw[:, :]), ALU.mult)
                    dve.wait_ge(e_sum, c + 1)
                    dve.tensor_tensor(state[:, u, HEADS:], tp_ps[0][:, 0:D + HEADS], carried[:, :], ALU.add)\
                        .then_inc(e_state, 1)
                    dve.drain()
                    dve.tensor_tensor(tot[:, :], state[:, u, HEADS:HEADS + D], selfv[:, :], ALU.add)
                    dve.tensor_tensor(totw[:, :], state[:, u, HEADS + D:], selfw[:, :], ALU.add)
                    dve.drain()
                    dve.reciprocal(totw[:, :], totw[:, :])
                    dve.drain()
                    dve.wait_ge(e_sc[u], 32 * i + 16)
                    dve.tensor_tensor(heads(outb[:, u, :]), heads(tot[:, :]), over_heads(totw[:, :]),
                                      ALU.mult).then_inc(e_out[u], 1)

            dve.wait_ge(has_in, 64)
            dve.tensor_tensor(has[:, :], cnt_n[:, :], seen_n[:, :], ALU.add)
            dve.drain()
            dve.tensor_scalar(has[:, :], has[:, :], 0.0, None, ALU.is_gt)
            dve.wait_ge(late_in, 128)
            dve.drain()

            def b_x(g, i, u):
                dve.wait_ge(b_xb, g + 1)
                dve.wait_ge(b_u, g + 1)
                for k in range(G):
                    dve.wait_ge(b_mm, 3 * g + k + 1)
                    last = dve.scalar_tensor_tensor(x1[:, u, k, :], half[(u * G + k) % 2 * 2][:, 0:D],
                                                    has[:, ds(g * G + k, 1)], xb[:, u, k, :],
                                                    ALU.mult, ALU.add)
                    last.then_inc(b_x1t, 1)
                dve.drain().then_inc(b_x1, 1)
                for k in range(G):
                    dve.bn_stats(stats[:, u, k, :], x1[:, u, k, :])
                dve.drain()
                for k in range(G):
                    last = dve.bn_aggr(mv[:, u, k, :], stats[:, u, k, :])
                last.then_inc(b_var, 1)

            def b_weigh(g, u):
                dve.wait_ge(b_sd, g + 1)
                dve.reciprocal(rs[:, u, :], sd[:, u, :])
                dve.drain()
                for k in range(G):
                    dve.tensor_scalar(zt[:, k, :], x1[:, u, k, :], mv[:, u, k, 0:1], rs[:, u, k:k + 1],
                                      ALU.subtract, ALU.mult)
                dve.tensor_scalar(gain[:, u, :], rs[:, u, :], 1.0, None, ALU.add)
                dve.scalar_tensor_tensor(shift[:, u, :], mv[:, u, :, 0], -1.0, rs[:, u, :], ALU.mult, ALU.mult)
                dve.drain().then_inc(b_gain, 1)
                for k in range(G):
                    dve.tensor_tensor_reduce(out=zt[:, k, :], in0=zt[:, k, :], in1=wrs[:, :], scale=1.0,
                                             scalar=0.0, op0=ALU.mult, op1=ALU.add,
                                             accum_out=wst[:, u, k:k + 1])
                dve.drain()
                dve.tensor_copy(weight[:, ds(g * G, G)], wst[:, u, :])
                dve.tensor_copy(rs_n[:, ds(g * G, G)], rs[:, u, :])
                dve.tensor_copy(mean_n[:, ds(g * G, G)], mv[:, u, :, 0])

            b_x(0, 0, 0)
            with dve.Fori(0, NGRP // 2) as i:
                b_x(i * 2 + 1, i, 1)
                b_weigh(i * 2, 0)
                b_x(i * 2 + 2, i + 1, 0)
                b_weigh(i * 2 + 1, 1)
            b_weigh(NGRP, 0)
            dve.drain()

            dve.tensor_scalar(weight[:, :], weight[:, :], brs[:, 0:1], None, ALU.add)
            dve.tensor_scalar(has[:, :], rs_n[:, :], 1.0, None, ALU.add)
            dve.drain()
            dve.reciprocal(has[:, :], has[:, :])
            for k in (2, 3):
                dve.tensor_copy(norm_s[:, :, k], weight[:, :])
            dve.drain()
            dve.tensor_tensor(norm_s[:, :, 0], has[:, :], rs_n[:, :], ALU.mult)
            dve.drain()
            dve.scalar_tensor_tensor(norm_s[:, :, 1], mean_n[:, :], -1.0, norm_s[:, :, 0], ALU.mult, ALU.mult)
            dve.drain().then_inc(norm_ready, 1)

            wbits = weight[:, 0:T + 1].bitcast(i32)
            dve.tensor_scalar(key_a[:, :], wbits, 31, -2 ** 31, ALU.arith_shift_right, ALU.bitwise_or)
            dve.drain()
            dve.tensor_tensor(key_b[:, :], wbits, key_a[:, :], ALU.bitwise_xor)
            dve.drain()
            dve.tensor_scalar(key_a[:, :], key_b[:, :], 16, 65535, ALU.logical_shift_right, ALU.bitwise_and)
            dve.tensor_scalar(key_b[:, :], key_b[:, :], 65535, None, ALU.bitwise_and)
            dve.drain()
            dve.tensor_copy(key[:, 0, :], key_a[:, :])
            dve.tensor_copy(key[:, 1, :], key_b[:, :])
            dve.memset(thr[:, :], 0.0)
            dve.drain()
            for k in range(2):
                dve.tensor_scalar(key[:, k, T:T + 1], key[:, k, T:T + 1], 1.0, live[:, :], ALU.add, ALU.mult)
            dve.drain()
            for k in range(2):
                dve.tensor_scalar(key[:, k, T:T + 1], key[:, k, T:T + 1], -1.0, None, ALU.add)
            dve.drain()

            def largest(level, keys):
                t = thr[:, level:level + 1]
                with dve.Fori(0, 16) as s:
                    dve.tensor_scalar(cand[:, :], t, bits[:, ds(s, 1)], None, ALU.add)
                    dve.drain()
                    dve.tensor_scalar(hit[:, :], keys, cand[:, 0:1], None, ALU.is_ge, ALU.add,
                                      accum_out=cntc[:, :])
                    dve.drain().then_inc(t_cnt, 1)
                    dve.wait_ge(t_sum, s + (16 * level + 1))
                    dve.tensor_scalar(step[:, :], half[1][:, 0:1], KK - 0.5, bits[:, ds(s, 1)],
                                      ALU.is_gt, ALU.mult)
                    dve.drain()
                    dve.tensor_tensor(t, t, step[:, :], ALU.add)
                    dve.drain()

            largest(0, key[:, 0, :])
            dve.tensor_scalar(hit[:, :], key[:, 0, :], thr[:, 0:1], FAR + 1, ALU.is_gt, ALU.mult)
            dve.tensor_scalar(tied[:, :], key[:, 0, :], thr[:, 0:1], None, ALU.is_equal)
            dve.tensor_scalar(key[:, 1, :], key[:, 1, :], 1.0, None, ALU.add)
            dve.drain()
            dve.tensor_tensor(keyl[:, :], tied[:, :], key[:, 1, :], ALU.mult)
            dve.drain()
            dve.scalar_tensor_tensor(keyl[:, :], keyl[:, :], -1.0, hit[:, :], ALU.add, ALU.add)
            dve.drain()
            largest(1, keyl[:, :])

            def summed(n, column):
                dve.tensor_copy(cntc[:, :], column)
                dve.drain().then_inc(t_cnt, 1)
                dve.wait_ge(t_sum, n + 1)
                return half[1][:, 0:1]

            dve.tensor_scalar(hit[:, :], keyl[:, :], thr[:, 1:2], None, ALU.is_gt, ALU.add,
                              accum_out=step[:, :])
            dve.tensor_scalar(tied[:, :], keyl[:, :], thr[:, 1:2], None, ALU.is_equal)
            dve.drain()
            dve.tensor_scalar(need[:, :], summed(32, step[:, :]), -1.0, float(KK), ALU.mult, ALU.add)
            dve.tensor_tensor_scan(rank[:, 0:T], tied[:, 0:T], zeros[:, 0:T], 0.0, ALU.add, ALU.add)
            dve.drain()
            dve.tensor_copy(step[:, :], rank[:, T - 1:T])
            dve.drain()
            dve.tensor_copy(off[:, 0:1], summed(33, step[:, :]))
            dve.tensor_copy(off[:, 1:2], summed(34, tied[:, T:T + 1]))
            dve.tensor_copy(off1[:, :], summed(35, step[:, :]))
            dve.drain()
            dve.scalar_tensor_tensor(rank[:, 0:T], rank[:, 0:T], off[:, 0:1], tied[:, 0:T],
                                     ALU.add, ALU.subtract)
            dve.tensor_tensor(rank[:, T:T + 1], off[:, 1:2], off1[:, :], ALU.add)
            dve.drain()
            dve.scalar_tensor_tensor(tied[:, :], rank[:, :], need[:, 0:1], tied[:, :], ALU.is_lt, ALU.mult)
            dve.drain()
            dve.tensor_tensor(hit[:, :], hit[:, :], tied[:, :], ALU.add)
            dve.drain()
            dve.tensor_tensor_scan(rank[:, :], hit[:, :], zeros[:, 0:T + 1], 0.0, ALU.add, ALU.add)
            dve.drain()
            dve.tensor_copy(off[:, 0:1], summed(36, rank[:, T:T + 1]))
            dve.drain()
            dve.scalar_tensor_tensor(rank[:, :], rank[:, :], off[:, 0:1], hit[:, :], ALU.add, ALU.subtract)
            dve.drain()
            dve.scalar_tensor_tensor(rank[:, :], rank[:, :], -FAR, hit[:, :], ALU.add, ALU.mult)
            dve.drain()
            dve.tensor_scalar(chpos[:, :], rank[:, :], FAR, None, ALU.add)
            dve.drain()
            for src_i, dest, n in ((chpos[:, :], slot_f, 7), (node[:, 0:T + 1], node_f, 8)):
                dve.tensor_scalar(key_a[:, :], src_i, (1 << n) - 1, None, ALU.bitwise_and)
                dve.tensor_scalar(key_b[:, :], src_i, n, None, ALU.logical_shift_right)
                dve.drain()
                dve.tensor_copy(dest[:, 0, :], key_a[:, :])
                dve.tensor_copy(dest[:, 1, :], key_b[:, :])
                dve.drain()

            def list_column(k, t, free):
                dve.wait_ge(ch_free, free)
                for s in range(2):
                    dve.tensor_scalar(oh_slot[:, k, s, :], iota[:, 0:P], slot_f[:, 0, t], node_f[:, s, t],
                                      ALU.is_equal, ALU.mult)
                dve.tensor_scalar(oh_col[:, k, :], iota[:, 0:FC], slot_f[:, 1, t], None, ALU.is_equal)\
                    .then_inc(ch_oh, 1)

            with dve.Fori(0, T // 4) as i:
                for k in range(4):
                    list_column(k, ds(i * 4 + k, 1), i * 4 + k + 1)
            for k in range(T // 4 * 4, T + 1):
                list_column(k % 4, slice(k, k + 1), k + 1)
            dve.tensor_scalar(past[:, :], iota[:, 0:FC], float(P), pcol[:, 0:1], ALU.mult, ALU.add)
            dve.drain()
            dve.tensor_scalar(past[:, :], past[:, :], KK - 0.5, FAR, ALU.is_gt, ALU.mult)
            dve.wait_ge(ch_done, 1)
            dve.drain()
            dve.tensor_tensor(past[:, :], sort_ps[0][:, 0:FC], past[:, :], ALU.add)
            dve.drain()
            dve.scalar_tensor_tensor(chosen[:, :], sort_ps[1][:, 0:FC], 256.0, past[:, :], ALU.mult, ALU.add)\
                .then_inc(ch_ready, 1)

            def f_norm(g, i, u):
                dve.wait_ge(f_in[u], 2 * FG * 16 * (i + 1))
                for c in range(FG):
                    last = dve.tensor_scalar(fz[:, u, c, :], fu[:, u, c, :], fn[:, u, c, 0:1],
                                             fn[:, u, c, 1:2], ALU.mult, ALU.add)
                last.then_inc(f_z, 1)

            def f_out(g, i, u):
                dve.wait_ge(f_sc[u], FG * 16 * i + 16)
                for c in range(FG):
                    dve.wait_ge(f_m2, FG * g + c + 1)
                    dve.tensor_tensor(fy[:, c % 2, :], half[2 + c % 2][:, 0:D], b2s[:, :], ALU.add)\
                        .then_inc(f_y, 1)
                    dve.drain()
                    last = dve.scalar_tensor_tensor(fo[:, u, c, :], fy[:, c % 2, :], fn[:, u, c, 2:3],
                                                    fu[:, u, c, :], ALU.mult, ALU.add)
                last.then_inc(f_o, 1)

            f_norm(0, 0, 0)
            r = (NFG - 1) // 2
            with dve.Fori(0, r) as i:
                f_norm(i * 2 + 1, i, 1)
                f_out(i * 2, i, 0)
                f_norm(i * 2 + 2, i + 1, 0)
                f_out(i * 2 + 1, i, 1)
            if NFG % 2 == 0:
                f_norm(NFG - 1, r, 1)
            f_out(2 * r, r, 0)
            if NFG % 2 == 0:
                f_out(NFG - 1, r, 1)


_INS = ["x", "src", "dst", "L0_gnn_Wq", "L0_gnn_bq", "L0_gnn_Wk", "L0_gnn_bk", "L0_gnn_Wv", "L0_gnn_bv",
        "L0_gnn_Wo", "L0_gnn_bo", "L0_ffn_wr", "L0_ffn_br", "L0_ffn_w1", "L0_ffn_b1", "L0_ffn_w2",
        "L0_ffn_b2"]


def kernel(**inputs):
    import numpy as np
    import concourse.bacc as bacc
    from concourse.bass_utils import run_bass_kernel_spmd

    nc = bacc.Bacc("TRN2", target_bir_lowering=False, num_devices=1)
    arrays, args = {}, []
    for name in _INS:
        a = np.ascontiguousarray(inputs[name])
        arrays[f"in_{name}"] = a
        args.append(nc.dram_tensor(f"in_{name}", a.shape, mybir.dt.from_np(a.dtype),
                                   kind="ExternalInput").ap())
    shape = arrays["in_x"].shape
    out = nc.dram_tensor("out", shape, f32, kind="ExternalOutput").ap()
    gnn_ffn_kernel(nc, *args, out)
    r = run_bass_kernel_spmd(nc, [arrays], core_ids=[0])
    return r.results[0]["out"]
```

```python
import concourse.bass as bass
from concourse import mybir
from concourse.alu_op_type import AluOpType as ALU
from contextlib import ExitStack

f32 = mybir.dt.float32
bf16 = mybir.dt.bfloat16
i32 = mybir.dt.int32
i16 = mybir.dt.int16
f16 = mybir.dt.float16
u16 = mybir.dt.uint16
ACT = mybir.ActivationFunctionType
AX = mybir.AxisListType.X
IDX = bass.IndirectOffsetOnAxis
ds = bass.ds

P = 128
D = 256
HEADS = 8
HD = D // HEADS
HID = 4 * D
EPS = 1e-5
BIG = 1e30
NONE = 65535
FAR = 70000.0
WS = 32.0


def gnn_ffn_kernel(nc, x, src, dst, Wq, bq, Wk, bk, Wv, bv, Wo, bo, wr, br, w1, b1, w2, b2, out):
    N = x.shape[0]
    E = src.shape[0]
    T = N // P
    REST = N - P * T
    G = 3
    NGRP = T // G
    assert T % (2 * G) == 0 and 0 < REST and REST % 16 == 0
    TC = T + G
    LO = 512
    HI = (N + LO - 1) // LO
    EP = 125
    EC = E // EP
    assert E == EP * EC and EC % 20 == 0
    JC = (-(-E // P) + 7) // 8 * 8
    JB = JC // 4
    assert JB <= P and JC <= 512
    LBASE = P
    LLEN = JC * P + 2 * P
    KK = max(1, N // 2) - 1
    FG = 4
    NFG = -(-KK // (FG * P))
    FC = NFG * FG
    KT = D // P
    HT = HID // P
    SCALE = HD ** -0.5

    qkv_t = nc.dram_tensor("qkv_t", [N, 3 * D], f32, kind="Internal").ap()
    attn_t = nc.dram_tensor("attn_t", [N, D], f32, kind="Internal").ap()
    cnt_t = nc.dram_tensor("cnt_t", [HI * LO, 1], f32, kind="Internal").ap()
    seen_t = nc.dram_tensor("seen_t", [HI * LO, 1], f32, kind="Internal").ap()
    lists = [nc.dram_tensor(f"list_{k}", [LLEN, 2], i32, kind="Internal").ap() for k in range(2)]
    reset_t = nc.dram_tensor("reset_t", [JC, P], f32, kind="Internal").ap()
    norm_t = nc.dram_tensor("norm_t", [N, 4], f32, kind="Internal").ap()

    def grouped(table, w):
        return table[0:P * T, :].rearrange("(p t) c -> p t c", t=T)

    with ExitStack() as ctx:
        def sb(name, shape, dt=f32):
            return ctx.enter_context(nc.sbuf_tensor(name, shape, dt))

        def sem(name):
            return ctx.enter_context(nc.semaphore(name))

        def pair(name):
            return [sem(f"{name}{u}") for u in range(2)]

        wqkv = sb("wqkv", [P, 2, KT, 3 * D], f16)
        wo = sb("wo", [P, KT, D])
        w1s = sb("w1s", [P, 2, KT, HID], f16)
        w2s = sb("w2s", [P, 2, HT, D], f16)
        bqkv = sb("bqkv", [P, 3 * D])
        bos = sb("bos", [P, D])
        b2s = sb("b2s", [P, D])
        b1s = sb("b1s", [P, HT])
        wrs = sb("wrs", [P, D])
        brs = sb("brs", [P, 1])
        ident = sb("ident", [P, P])
        iota = sb("iota", [P, LO], i16)
        digits = sb("digits", [P, 17])
        bits = sb("bits", [P, 16])
        from_here = sb("from_here", [P, P], bf16)
        ones_b = sb("ones_b", [P, P], bf16)
        zeros_b = sb("zeros_b", [P, LO], bf16)
        before = sb("before", [P, P])
        ones = sb("ones", [P, P])
        zeros = sb("zeros", [P, LO])
        eps = sb("eps", [P, 1])
        opened = sb("opened", [16, 16, 16])
        node = sb("node", [P, TC], i32)

        SPACE = 18432
        space = sb("space", [P, SPACE])
        taken = {"early": 0, "late": 0}

        def in_space(when, shape, dt=f32, each=1):
            width = 1
            for n in shape[1:]:
                width *= n
            a = taken[when]
            taken[when] += (width + each - 1) // each
            assert taken[when] <= SPACE
            v = space[0:shape[0], a:taken[when]]
            if dt != f32:
                v = v.bitcast(dt)[:, 0:width]
            names = "abc"[0:len(shape) - 1]
            if len(names) > 1:
                sizes = {n: c for n, c in zip(names, shape[1:])}
                v = v.rearrange(f"p ({' '.join(names)}) -> p {' '.join(names)}", **sizes)
            return v

        def early(*shape, dt=f32, each=1):
            return in_space("early", shape, dt, each)

        def late(*shape, dt=f32, each=1):
            return in_space("late", shape, dt, each)

        bank = [ctx.enter_context(nc.psum_tensor(f"qkv_ps{k}", [P, 1024], f32)) for k in range(2)]
        bank2 = [ctx.enter_context(nc.psum_tensor(f"ps{k}", [P, 512], f32)) for k in range(4)]
        qkv_ps = bank
        tp_ps = bank2[0:2]
        sort_ps = bank2[2:4]
        b_tp_ps = bank2[0:3]
        rank_ps = [[b[:, :] for b in sort_ps], [b[:, 0:512] for b in bank]]
        half = [bank[0][:, 0:512], bank[0][:, 512:1024], bank[1][:, 0:512], bank[1][:, 512:1024]]

        none = early(P, LLEN * 2 // P, dt=i32)
        edge = early(EP, 2, EC, dt=i32)
        edge_f = early(EP, 2, EC)
        is_self = early(EP, EC)
        lo_i = early(EP, EC, dt=i32)
        hi_i = early(EP, EC, dt=i32)
        lo_f = early(EP, EC)
        hi_f = early(EP, EC)
        oh_hi = early(EP, 4, P, dt=bf16, each=2)
        oh_lo = early(EP, 4, LO, dt=bf16, each=2)
        cnt_s = early(HI, LO)
        W = max(EC, JC)
        digit_i = early(P, W, dt=i32)
        digit = early(P, W)
        onehot = early(P, 2, W, dt=bf16, each=2)
        upto = early(P, W)
        place = early(P, W)
        pos = early(P, W)
        pos_i = early(P, W, dt=i32)
        base = sb("base", [P, 1])
        pay = early(P, W, 2, dt=i32)
        row_i = early(P, JC, dt=i32)
        idx_blk = sb("idx_blk", [P, 2, 10], i32)
        pay_blk = sb("pay_blk", [P, 2, 10, 2], i32)
        groups_f = sb("groups_f", [P, 1])
        groups_i = sb("groups_i", [P, 1], i32)
        lst = early(JB, 4, 2 * P, dt=i32)
        lst_f = early(JB, 2, 4, P)
        near = early(JB, 2, 4, 2 * P, dt=i32)
        near_f = early(JB, 2, 4, P)
        reset_s = early(JB, 4, P)

        rows_in = sb("rows_in", [P, 4, G, D])
        xg, ag = rows_in[:, 0:2, :, :], rows_in[:, 2:4, :, :]
        stats = sb("stats", [P, 2, G, 6])
        mv = sb("mv", [P, 2, G, 2])
        sd = sb("sd", [P, 2, G])
        rs = sb("rs", [P, 2, G])
        h = sb("h", [P, 2, G, D])
        ht = sb("ht", [P, 2, G, D])
        ht2 = ht[:, :, :, :].rearrange("p u g d -> p (u g d)").bitcast(f16)\
            .rearrange("p (u s g d) -> p u s g d", u=2, s=2, g=G)
        qkv = sb("qkv", [P, 2, G, 3 * D])
        wqkv_f = qkv[:, :, :, :].rearrange("p u g d -> p (u g d)")[:, 0:KT * 3 * D]\
            .rearrange("p (k n) -> p k n", k=KT)

        col_row = sb("col_row", [P, JC + 2])
        col_last = sb("col_last", [P, JC + 2])
        col_carry = sb("col_carry", [P, JC + 2])
        col_next = sb("col_next", [P, JC + 2])
        idx_all = sb("idx_all", [P, JC + 2, 3], i32)
        gidx = sb("gidx", [P, 2, 3], i32)
        sidx = sb("sidx", [P, 2, 1], i32)
        ends = sb("ends", [P, 4, 3 * D])
        rowg, colg = ends[:, 0:2, :], ends[:, 2:4, :]
        cntg = sb("cntg", [P, 2, 1])
        row_bc = sb("row_bc", [P, 2, P, 2], i32)
        reset_bc = sb("reset_bc", [HEADS, 2, P])
        qk = sb("qk", [P, 2, D])
        same = sb("same", [P, 2, P])
        lastm = sb("lastm", [P, 2, P])
        carrym = sb("carrym", [P, 2, P])
        no_self = sb("no_self", [P, 1])
        raw = sb("raw", [P, 2, HEADS])
        sc = sb("sc", [P, 2, 2, HEADS])
        smax = sb("smax", [P, HEADS])
        run = sb("run", [HEADS, 2, P])
        runt = sb("runt", [P, HEADS])
        expo = sb("expo", [P, 3, HEADS])
        ex = sb("ex", [P, 3, HEADS])
        pv = sb("pv", [P, D + HEADS])
        selfv = sb("selfv", [P, D])
        selfw = sb("selfw", [P, HEADS])
        carried = sb("carried", [P, D + HEADS])
        state = sb("state", [P, 2, HEADS + D + HEADS])
        tot = sb("tot", [P, D])
        totw = sb("totw", [P, HEADS])
        outb = sb("outb", [P, 2, D])

        fh_at = late(P, 2 * HT * FG * P)
        fh = fh_at.bitcast(f16).rearrange("p (u s k n) -> p u s k n", u=2, s=2, k=HT)
        after_fh, taken["late"] = taken["late"], 0
        xb = late(P, 2, G, D)
        x1 = late(P, 2, G, D)
        ug = late(P, 2, G, D)
        zt = late(P, 2, G, D)
        taken["late"] = after_fh
        shift = sb("shift", [P, 2, G])
        gain = sb("gain", [P, 2, G])
        wst = sb("wst", [P, 2, G])
        cnt_n = sb("cnt_n", [P, TC])
        seen_n = sb("seen_n", [P, TC])
        has = late(P, TC)
        mean_n = late(P, TC)
        rs_n = late(P, TC)
        weight_at = late(P, 2 * G + TC)
        weight = weight_at[:, 2 * G:2 * G + TC]
        norm_s = late(P, TC, 4)

        before_w = taken["late"]
        w1f = late(P, KT, HID)
        w2f = late(P, HT, D)
        taken["late"] = before_w

        key_a = late(P, T + 1, dt=i32)
        key_b = late(P, T + 1, dt=i32)
        key = late(P, 2, T + 1)
        keyl = late(P, T + 1)
        hit = late(P, T + 1)
        tied = late(P, T + 1)
        rank = late(P, T + 1)
        chpos = late(P, T + 1, dt=i32)
        thr = sb("thr", [P, 2])
        cand = sb("cand", [P, 1])
        cntc = sb("cntc", [P, 1])
        step = sb("step", [P, 1])
        need = sb("need", [P, 1])
        off = sb("off", [P, 2])
        live = sb("live", [P, 1])
        pcol = sb("pcol", [P, 1])
        off1 = sb("off1", [P, 1])
        slot_f = late(P, 2, T + 1)
        node_f = late(P, 2, T + 1)
        oh_slot = late(P, 4, 2, P, dt=bf16, each=2)
        oh_col = late(P, 4, FC, dt=bf16, each=2)
        past = late(P, FC)

        chosen = late(P, FC, dt=i32)
        fidx = sb("fidx", [P, 2, FG], i32)
        fu = rows_in[:, :, :, :].rearrange("p a b c -> p (a b c)")[:, 0:2 * FG * D]\
            .rearrange("p (u c d) -> p u c d", u=2, c=FG)
        fn = sb("fn", [P, 2, FG, 4])
        spent = qkv[:, :, :, :].rearrange("p a b c -> p (a b c)")
        fz, fo = (spent[:, k * 2 * FG * D:(k + 1) * 2 * FG * D].rearrange("p (u c d) -> p u c d", u=2, c=FG)
                  for k in range(2))
        fzt = ends[:, :, :].rearrange("p a c -> p (a c)")[:, 0:2 * KT * FG * P].bitcast(f16)\
            .rearrange("p (u s k n) -> p u s k n", u=2, s=2, k=KT)
        up_ps = [*half[0:2], *[b[:, :] for b in sort_ps]]
        fy = late(P, 2, D)

        consts = sem("consts")
        aside = sem("aside")
        edges_in = sem("edges_in")
        wqkv_in = sem("wqkv_in")
        wqkv_hi = sem("wqkv_hi")
        wqkv_lo = sem("wqkv_lo")
        late_in = sem("late_in")
        prefilled = sem("prefilled")
        hist_oh = sem("hist_oh")
        hist_free = sem("hist_free")
        hist_done = sem("hist_done")
        cnt_ready = sem("cnt_ready")
        cnt_stored = sem("cnt_stored")
        sort_oh = sem("sort_oh")
        sort_mm = sem("sort_mm")
        pos_ready = sem("pos_ready")
        groups_ready = sem("groups_ready")
        scat = [pair(f"scat{k}_") for k in range(4)]
        scattered = sem("scattered")
        list_in = sem("list_in")
        list_f = sem("list_f")
        list_t = sem("list_t")
        reset_ready = sem("reset_ready")
        reset_stored = sem("reset_stored")
        cols_ready = sem("cols_ready")

        ax_in = pair("ax_in")
        a_var = sem("a_var")
        a_sd = sem("a_sd")
        a_h = sem("a_h")
        a_tp = sem("a_tp")
        a_hi = sem("a_hi")
        a_ht = sem("a_ht")
        a_mm = sem("a_mm")
        a_ev = sem("a_ev")
        a_stored = pair("a_stored")

        e_row_in = pair("e_row_in")
        e_in = pair("e_in")
        e_smax = sem("e_smax")
        e_used = sem("e_used")
        e_idx = sem("e_idx")
        e_st = sem("e_st")
        e_run = sem("e_run")
        e_rt = sem("e_rt")
        e_runt = sem("e_runt")
        e_max = sem("e_max")
        e_cmax = sem("e_cmax")
        e_expo = sem("e_expo")
        e_ex = sem("e_ex")
        e_pv = sem("e_pv")
        e_sum = sem("e_sum")
        e_state = sem("e_state")
        e_out = pair("e_out")
        e_sc = pair("e_sc")
        e_end = sem("e_end")

        has_in = sem("has_in")
        b_in = pair("b_in")
        b_xin = pair("b_xin")
        b_xb = sem("b_xb")
        b_tp = sem("b_tp")
        b_at = sem("b_at")
        b_mm = sem("b_mm")
        b_x1 = sem("b_x1")
        b_x1t = sem("b_x1t")
        b_var = sem("b_var")
        b_sd = sem("b_sd")
        b_gain = sem("b_gain")
        b_z = sem("b_z")
        b_u = sem("b_u")
        b_fin = sem("b_fin")
        b_stored = pair("b_stored")

        t_cnt = sem("t_cnt")
        t_sum = sem("t_sum")
        norm_ready = sem("norm_ready")
        norm_stored = sem("norm_stored")
        ch_oh = sem("ch_oh")
        ch_free = sem("ch_free")
        ch_done = sem("ch_done")
        ch_ready = sem("ch_ready")

        w_in = sem("w_in")
        w_hi = sem("w_hi")
        w_lo = sem("w_lo")
        f_in = pair("f_in")
        f_z = sem("f_z")
        f_tp = sem("f_tp")
        f_zh = sem("f_zh")
        f_zt = sem("f_zt")
        f_m1 = sem("f_m1")
        f_g = sem("f_g")
        f_h = sem("f_h")
        f_m2 = sem("f_m2")
        f_y = sem("f_y")
        f_o = sem("f_o")
        f_sc = pair("f_sc")

        cuts = [0, NGRP // 2 * 27 // 65, NGRP // 2 * 39 // 65, NGRP // 2 * 51 // 65]
        block = ctx.enter_context(nc.Block())

        @block.sync
        def _(sp):
            for k, s in enumerate((*a_stored, *b_stored)):
                sp.dma_start(opened[:, k, :], x[0:16, 0:16]).then_inc(s, 16)
            for k, e in enumerate((src, dst)):
                sp.dma_start(edge[:, k, :], e.rearrange("(p c) -> p c", c=EC)).then_inc(edges_in, 16)
            for k, w in enumerate((Wq, Wk, Wv)):
                sp.dma_start(wqkv_f[:, :, k * D:(k + 1) * D],
                             w.rearrange("(k p) n -> p k n", p=P)).then_inc(wqkv_in, 16)
            for k, b in enumerate((bq, bk, bv)):
                sp.dma_start(bqkv[:, k * D:(k + 1) * D],
                             b.rearrange("(a n) -> a n", a=1).partition_broadcast(P)).then_inc(wqkv_in, 16)

            sp.wait_ge(consts, 1)
            for l in lists:
                sp.dma_start(l.rearrange("(p c) k -> p (c k)", p=P), none[:, :]).then_inc(prefilled, 16)
            sp.dma_start(seen_t.rearrange("(p c) k -> p (c k)", p=HI), zeros[0:HI, :]).then_inc(prefilled, 16)

            def load_x(g, u, tail=False):
                if tail:
                    sp.dma_start(xg[0:REST, u, 0, :], x[P * T:N, :]).then_inc(ax_in[u], 16)
                else:
                    sp.dma_start(xg[:, u, :, :],
                                 grouped(x, D)[:, ds(g * G, G), :]).then_inc(ax_in[u], 16)

            def store_qkv(g, u, tail=False):
                if tail:
                    sp.dma_start(qkv_t[P * T:N, :], qkv[0:REST, u, 0, :]).then_inc(a_stored[u], 16)
                    sp.dma_start(attn_t[P * T:N, :], qkv[0:REST, u, 0, 2 * D:]).then_inc(a_stored[u], 16)
                else:
                    sp.dma_start(grouped(qkv_t, 3 * D)[:, ds(g * G, G), :], qkv[:, u, :, :])\
                      .then_inc(a_stored[u], 16)
                    sp.dma_start(grouped(attn_t, D)[:, ds(g * G, G), :], qkv[:, u, :, 2 * D:])\
                      .then_inc(a_stored[u], 16)

            def a_group(i, u, tail_next=False, load=True):
                g = 2 * i + u
                if load:
                    sp.wait_ge(a_h, g + 2)
                    load_x(g + 3, 1 - u, tail_next)
                sp.wait_ge(a_ev, 3 * g + 5)
                store_qkv(g, u)

            def a_loop(lo, hi):
                with sp.Fori(lo, hi) as i:
                    for u in range(2):
                        a_group(i, u)

            def load_list(k, p):
                sp.wait_ge(scattered, p)
                sp.dma_start(lst[:, :, :],
                             lists[k][LBASE:LBASE + JC * P, :].rearrange("(b j e) k -> j b (e k)", b=4, e=P))\
                  .then_inc(list_in, 16)

            load_x(0, 0)
            load_x(1, 1)
            sp.wait_ge(a_h, 1)
            load_x(2, 0)
            a_loop(cuts[0], cuts[1])
            sp.wait_ge(cnt_ready, 1)
            sp.dma_start(cnt_t.rearrange("(p c) k -> p (c k)", p=HI), cnt_s[:, :]).then_inc(cnt_stored, 16)
            load_list(0, 1)
            a_loop(cuts[1], cuts[2])
            load_list(1, 2)
            a_loop(cuts[2], cuts[3])
            load_list(0, 3)
            a_loop(cuts[3], NGRP // 2 - 2)
            a_group(NGRP // 2 - 2, 0)
            a_group(NGRP // 2 - 2, 1, tail_next=True)
            for u in range(2):
                a_group(NGRP // 2 - 1, u, load=False)
            sp.wait_ge(a_ev, 3 * NGRP + 3)
            store_qkv(NGRP, 0, tail=True)
            load_list(1, 4)
            for k, o in enumerate((-1, 1)):
                sp.dma_start(near[:, k, :, :],
                             lists[1][LBASE + o:LBASE + o + JC * P, :]
                             .rearrange("(b j e) k -> j b (e k)", b=4, e=P)).then_inc(list_in, 16)
            sp.wait_ge(reset_ready, 1)
            sp.dma_start(reset_t.rearrange("(b j) e -> j b e", b=4), reset_s[:, :, :])\
              .then_inc(reset_stored, 16)
            sp.wait_ge(reset_stored, 16)

            groups = sp.value_load(groups_i[0:1, 0:1], min_val=1, max_val=JC // 8)
            rows_of = lists[1].rearrange("(j e) k -> j (e k)", e=P)

            def load_rows(c, u, reset_row):
                sp.wait_ge(e_run, c + 1)
                sp.dma_start(row_bc[:, u, :, :].rearrange("p e k -> p (e k)"),
                             rows_of[ds(c + 1, 1), :].partition_broadcast(P)).then_inc(e_row_in[u], 16)
                sp.dma_start(reset_bc[:, u, :],
                             reset_t[ds(reset_row, 1), :].partition_broadcast(HEADS))\
                  .then_inc(e_row_in[u], 16)

            with sp.Fori(0, groups * 4) as i:
                for u in range(2):
                    load_rows(i * 2 + u, u, i * 2 + u)
            load_rows(groups * 8, 0, 0)

            sp.wait_ge(e_end, 1)
            for k, (t, s) in enumerate(((cnt_t, cnt_n), (seen_t, seen_n))):
                sp.dma_start(s[:, 0:T], t[0:P * T, :].rearrange("(p t) c -> p (t c)", t=T))\
                  .then_inc(has_in, 16)
                sp.dma_start(s[0:REST, T:T + 1], t[P * T:N, :]).then_inc(has_in, 16)

            def load_b(g, u, tail=False, first=False):
                if not first:
                    sp.wait_ge(b_tp, 3 * g - 3)
                if tail:
                    sp.dma_start(ag[0:REST, u, 0, :], attn_t[P * T:N, :]).then_inc(b_in[u], 16)
                else:
                    sp.dma_start(ag[:, u, :, :], grouped(attn_t, D)[:, ds(g * G, G), :]).then_inc(b_in[u], 16)
                if not first:
                    sp.wait_ge(b_xb, g - 1)
                if tail:
                    sp.dma_start(xg[0:REST, u, 0, :], x[P * T:N, :]).then_inc(b_xin[u], 16)
                else:
                    sp.dma_start(xg[:, u, :, :], grouped(x, D)[:, ds(g * G, G), :]).then_inc(b_xin[u], 16)

            for u in range(2):
                load_b(u, u, first=True)
            with sp.Fori(0, NGRP // 2 - 1) as i:
                for u in range(2):
                    load_b(i * 2 + (u + 2), u)
            load_b(NGRP, 0, tail=True)

            sp.wait_ge(norm_ready, 1)
            sp.dma_start(grouped(norm_t, 4), norm_s[:, 0:T, :]).then_inc(norm_stored, 16)
            sp.dma_start(norm_t[P * T:N, :], norm_s[0:REST, T, :]).then_inc(norm_stored, 16)

        @block.gpsimd
        def _(pool):
            for k, s in enumerate((*sum(scat, []), *e_sc, *f_sc)):
                pool.dma_start(opened[:, 4 + k, :], x[0:16, 0:16]).then_inc(s, 16)
            table_end = pool.to_reg(N - 1)
            list_end = pool.to_reg(LLEN - 1)

            def alone():
                pool.sem_inc(aside, 1)

            pool.iota(iota[:, :], [[1, LO]], base=0, channel_multiplier=0)
            pool.memset(ones_b[:, :], 1.0)
            pool.memset(zeros_b[:, :], 0.0)
            pool.memset(zeros[:, :], 0.0)
            pool.memset(ones[:, :], 1.0)
            pool.memset(eps[:, :], EPS)
            pool.memset(none[:, :], NONE)
            pool.memset(ident[:, :], 0.0)
            pool.memset(from_here[:, :], -1.0)
            pool.memset(before[:, :], 1.0)
            pool.iota(digits[:, :], [[1, 17]], base=0, channel_multiplier=0,
                      allow_small_or_imprecise_dtypes=True)
            for k in range(16):
                pool.memset(bits[:, k:k + 1], float(1 << (15 - k)))
            pool.iota(node[:, 0:T], [[1, T]], base=0, channel_multiplier=T)
            pool.iota(node[:, T:TC], [[0, G]], base=P * T, channel_multiplier=1)
            pool.drain()
            pool.affine_select(out=ident[:, :], in_=ident[:, :], compare_op=ALU.not_equal, fill=1.0,
                               base=0, pattern=[[-1, P]], channel_multiplier=1)
            pool.affine_select(out=from_here[:, :], in_=from_here[:, :], compare_op=ALU.is_ge, fill=0.0,
                               base=0, pattern=[[-1, P]], channel_multiplier=1)
            pool.affine_select(out=before[:, :], in_=before[:, :], compare_op=ALU.is_gt, fill=0.0,
                               base=0, pattern=[[1, P]], channel_multiplier=-1)
            for t in (ends, rows_in, cntg, fn, cnt_n, seen_n):
                pool.memset(t[:], 0.0)
            pool.iota(pcol[:, :], [[0, 1]], base=0, channel_multiplier=1,
                      allow_small_or_imprecise_dtypes=True)
            pool.affine_select(out=live[:, :], in_=ones[:, 0:1], compare_op=ALU.is_gt, fill=0.0,
                               base=REST, pattern=[[0, 1]], channel_multiplier=-1)
            pool.drain().then_inc(consts, 1)

            pool.wait_ge(prefilled, 48)
            pool.wait_ge(pos_ready, 1)

            def scatter_block(k, u, start, width, n, count, target):
                pool.wait_ge(scat[k][u], count + 16)
                pool.tensor_copy(idx_blk[0:n, u, 0:width], pos_i[0:n, ds(start, width)])
                pool.tensor_copy(pay_blk[0:n, u, 0:width, :], pay[0:n, ds(start, width), :])
                pool.drain()
                for c in range(width):
                    pool.indirect_dma_start(target, IDX(ap=idx_blk[0:n, u, c:c + 1], axis=0),
                                            pay_blk[0:n, u, c, :], None,
                                            bounds_check=list_end, oob_is_err=False)\
                        .then_inc(scat[k][u], 16)

            with pool.Fori(0, EC // 20) as i:
                for u in range(2):
                    scatter_block(0, u, i * 20 + u * 10, 10, EP, i * 160, lists[0])
            for u in range(2):
                pool.wait_ge(scat[0][u], EC // 20 * 160 + 16)
            pool.sem_inc(scattered, 1)

            pool.wait_ge(groups_ready, 1)
            groups = pool.value_load(groups_i[0:1, 0:1], min_val=1, max_val=JC // 8)
            for k in range(1, 4):
                pool.wait_ge(pos_ready, k + 1)
                with pool.Fori(0, groups) as i:
                    for u in range(2):
                        scatter_block(k, u, i * 8 + u * 4, 4, P, i * 64, lists[k % 2])
                for u in range(2):
                    pool.wait_ge(scat[k][u], groups * 64 + 16)
                pool.sem_inc(scattered, 1)

            def index(j, u):
                pool.tensor_copy(gidx[:, u, :], idx_all[:, ds(j, 1), :].rearrange("p a k -> p (a k)"))\
                    .then_inc(e_idx, 1)

            def gather(u):
                for t, k, dest in ((cnt_t, 0, cntg[:, u, :]), (qkv_t, 0, rowg[:, u, :]),
                                   (qkv_t, 1, colg[:, u, :])):
                    pool.indirect_dma_start(dest, None, t, IDX(ap=gidx[:, u, k:k + 1], axis=0),
                                            bounds_check=table_end, oob_is_err=False)\
                        .then_inc(e_in[u], 16)

            pool.wait_ge(cols_ready, 1)
            pool.wait_ge(cnt_stored, 16)
            for u in range(2):
                pool.wait_ge(a_stored[u], 32 * (NGRP // 2 + (u == 0)) + 16)
                index(u, u)
                pool.wait_ge(e_idx, u + 1)
                alone()
                gather(u)
            with pool.Fori(0, groups * 4) as i:
                for u in range(2):
                    c = i * 2 + u
                    pool.wait_ge(e_used, c + 1)
                    pool.wait_ge(e_sc[u], i * 32 + 16)
                    pool.tensor_copy(sidx[:, u, :], idx_all[:, ds(c, 1), 2])
                    index(c + 2, u)
                    pool.wait_ge(e_idx, c + 3)
                    alone()
                    gather(u)
                    pool.wait_ge(e_out[u], i + 2)
                    alone()
                    for t, s in ((attn_t, outb[:, u, :]), (seen_t, ones[:, 0:1])):
                        pool.indirect_dma_start(t, IDX(ap=sidx[:, u, :], axis=0), s, None,
                                                bounds_check=table_end, oob_is_err=False)\
                            .then_inc(e_sc[u], 16)
            for u in range(2):
                pool.wait_ge(e_sc[u], groups * 128 + 16)
                pool.wait_ge(e_in[u], groups * 192 + 48)
            pool.sem_inc(e_end, 1)

            def b_group(i, u):
                g = 2 * i + u
                pool.wait_ge(b_xin[u], 16 * i + 16)
                pool.wait_ge(b_x1, g + 1)
                pool.tensor_tensor(xb[:, u, :, :], xg[:, u, :, :],
                                   bos[:, :].unsqueeze(1).to_broadcast([P, G, D]), ALU.add)\
                    .then_inc(b_xb, 1)

            pool.wait_ge(late_in, 96)
            with pool.Fori(0, NGRP // 2) as i:
                for u in range(2):
                    b_group(i, u)
            b_group(NGRP // 2, 0)

            def f_gather(g, i, u):
                pool.wait_ge(f_sc[u], i * (FG * 16) + 16)
                alone()
                pool.tensor_copy(fidx[:, u, :], chosen[:, ds(g * FG, FG)])
                pool.drain()
                for c in range(FG):
                    for t, dest in ((out, fu[:, u, c, :]), (norm_t, fn[:, u, c, :])):
                        pool.indirect_dma_start(dest, None, t, IDX(ap=fidx[:, u, c:c + 1], axis=0),
                                                bounds_check=table_end, oob_is_err=False)\
                            .then_inc(f_in[u], 16)

            def f_scatter(g, u):
                pool.wait_ge(f_o, g + 1)
                alone()
                for c in range(FG):
                    pool.indirect_dma_start(out, IDX(ap=fidx[:, u, c:c + 1], axis=0),
                                            fo[:, u, c, :], None,
                                            bounds_check=table_end, oob_is_err=False)\
                        .then_inc(f_sc[u], 16)

            pool.wait_ge(ch_ready, 1)
            pool.wait_ge(norm_stored, 32)
            for u in range(2):
                pool.wait_ge(b_stored[u], 16 * (NGRP // 2 + (u == 0)) + 16)
            f_gather(0, 0, 0)
            with pool.Fori(0, (NFG - 1) // 2) as i:
                f_gather(i * 2 + 1, i, 1)
                f_scatter(i * 2, 0)
                f_gather(i * 2 + 2, i + 1, 0)
                f_scatter(i * 2 + 1, 1)
            r = (NFG - 1) // 2
            if NFG % 2 == 0:
                f_gather(NFG - 1, r, 1)
            f_scatter(2 * r, 0)
            if NFG % 2 == 0:
                f_scatter(NFG - 1, 1)
            for u in range(2):
                pool.wait_ge(f_sc[u], FG * 16 * ((NFG + 1 - u) // 2) + 16)

        @block.scalar
        def _(act):
            act.dma_start(wo[:, :, :], Wo.rearrange("(k p) n -> p k n", p=P)).then_inc(late_in, 16)
            act.dma_start(b1s[:, :], b1.rearrange("(k p) -> p k", p=P),
                          allow_slow_non_contiguous=True).then_inc(late_in, 16)
            act.dma_start(brs[:, :], br.rearrange("(a n) -> a n", a=1).partition_broadcast(P))\
                .then_inc(late_in, 16)
            for s, v in ((bos, bo), (b2s, b2)):
                act.dma_start(s[:, :], v.rearrange("(a n) -> a n", a=1).partition_broadcast(P))\
                    .then_inc(late_in, 16)
            act.dma_start(wrs[:, :], wr.rearrange("n a -> a n").partition_broadcast(P))\
                .then_inc(late_in, 16)
            act.sem_inc(b_u, 2)
            act.sem_inc(b_z, 1)
            act.sem_inc(b_at, 3)
            act.wait_ge(consts, 1)

            act.wait_ge(wqkv_in, 96)
            act.activation(wqkv[:, 0, :, :], wqkv_f[:, :, :], ACT.Copy, scale=WS).then_inc(wqkv_hi, 1)

            def a_high(g, u, k):
                act.wait_ge(a_tp, 3 * g + k + 1)
                act.activation(ht2[:, u, 0, k, :], tp_ps[(u * G + k) % 2][:, 0:D], ACT.Copy)\
                    .then_inc(a_hi, 1)

            def a_dev(g, u):
                act.wait_ge(a_var, g + 1)
                act.activation(sd[:, u, :], mv[:, u, :, 1], ACT.Sqrt, bias=eps[:, 0:1]).then_inc(a_sd, 1)

            def a_group(g, u, ahead=True):
                a_high(g + 1, 1 - u, 0)
                if ahead:
                    a_dev(g + 2, u)
                a_high(g + 1, 1 - u, 1)
                a_high(g + 1, 1 - u, 2)

            a_dev(0, 0)
            a_dev(1, 1)
            for k in range(G):
                a_high(0, 0, k)
            with act.Fori(0, NGRP // 2 - 1) as i:
                for u in range(2):
                    a_group(i * 2 + u, u)
            a_group(NGRP - 2, 0)
            a_group(NGRP - 1, 1, ahead=False)

            act.wait_ge(groups_ready, 1)
            groups = act.value_load(groups_i[0:1, 0:1], min_val=1, max_val=JC // 8)
            with act.Fori(0, groups * 4) as i:
                for u in range(2):
                    c = i * 2 + u
                    act.wait_ge(e_rt, c + 1)
                    act.activation(runt[:, :], half[1][:, 0:HEADS], ACT.Copy).then_inc(e_runt, 1)
                    act.wait_ge(e_max, c + 1)
                    act.activation(state[:, u, 0:HEADS], half[2][:, 0:HEADS], ACT.Copy)\
                        .then_inc(e_cmax, 1)
                    act.wait_ge(e_expo, c + 1)
                    act.activation(ex[:, :, :], expo[:, :, :], ACT.Exp).then_inc(e_ex, 1)

            act.wait_ge(e_end, 1)
            act.dma_start(w1f[:, :, :], w1.rearrange("(k p) n -> p k n", p=P)).then_inc(w_in, 16)
            act.dma_start(w2f[:, :, :], w2.rearrange("(k p) n -> p k n", p=P)).then_inc(w_in, 16)
            act.wait_ge(w_in, 32)
            act.activation(w1s[:, 0, :, :], w1f[:, :, :], ACT.Copy, scale=WS).then_inc(w_hi, 1)
            act.activation(w2s[:, 0, :, :], w2f[:, :, :], ACT.Copy, scale=WS).then_inc(w_hi, 1)

            def b_dev(g, u):
                act.wait_ge(b_var, g + 1)
                act.activation(sd[:, u, :], mv[:, u, :, 1], ACT.Sqrt, bias=eps[:, 0:1]).then_inc(b_sd, 1)

            def b_ht(g, u):
                for k in range(G):
                    act.wait_ge(b_tp, 3 * g + k + 1)
                    act.activation(ht[:, u, k, :], b_tp_ps[k][:, 0:D], ACT.Copy).then_inc(b_at, 1)

            def b_norm(g, u):
                act.wait_ge(b_gain, g + 1)
                for k in range(G):
                    last = act.activation(zt[:, u, k, :], x1[:, u, k, :], ACT.Identity,
                                          bias=shift[:, u, k:k + 1], scale=rs[:, u, k:k + 1])
                last.then_inc(b_z, 1)

            def b_sum(g, i, u, tail=False):
                act.wait_ge(b_stored[u], 16 * i + 16)
                for k in range(G):
                    last = act.activation(ug[:, u, k, :], x1[:, u, k, :], ACT.Identity,
                                          bias=shift[:, u, k:k + 1], scale=gain[:, u, k:k + 1])
                last.then_inc(b_u, 1)
                act.wait_ge(b_u, g + 3)
                if tail:
                    act.dma_start(out[P * T:N, :], ug[0:REST, u, 0, :]).then_inc(b_stored[u], 16)
                else:
                    act.dma_start(grouped(out, D)[:, ds(g * G, G), :], ug[:, u, :, :])\
                        .then_inc(b_stored[u], 16)

            b_ht(0, 0)
            b_ht(1, 1)
            b_dev(0, 0)
            r = NGRP // 2 - 1
            with act.Fori(0, r) as i:
                for u in range(2):
                    g = i * 2 + u
                    b_ht(g + 2, u)
                    b_norm(g, u)
                    b_dev(g + 1, 1 - u)
                    b_sum(g, i, u)
            b_ht(NGRP, 0)
            b_norm(NGRP - 2, 0)
            b_dev(NGRP - 1, 1)
            b_sum(NGRP - 2, r, 0)
            b_norm(NGRP - 1, 1)
            b_dev(NGRP, 0)
            b_sum(NGRP - 1, r, 1)
            b_norm(NGRP, 0)
            b_sum(NGRP, r + 1, 0, tail=True)

            def f_trans(g, u):
                for c in range(FG):
                    act.wait_ge(f_tp, FG * g + c + 1)
                    act.activation(fzt[:, u, 0, :, c * P:(c + 1) * P],
                                   tp_ps[c % 2][:, 0:D].rearrange("p (k n) -> p k n", k=KT), ACT.Copy)\
                        .then_inc(f_zh, 1)

            def f_gelu(g, u):
                for k in range(HT):
                    act.wait_ge(f_m1, HT * g + k + 1)
                    for dest in (fh[:, u, 0, k, :], up_ps[k % 4]):
                        last = act.activation(dest, up_ps[k % 4], ACT.Gelu_apprx_tanh,
                                              bias=b1s[:, k:k + 1], scale=1 / WS)
                    last.then_inc(f_g, 1)

            f_trans(0, 0)
            r = (NFG - 1) // 2
            with act.Fori(0, r) as i:
                for u in range(2):
                    f_gelu(i * 2 + u, u)
                    f_trans(i * 2 + (u + 1), 1 - u)
            f_gelu(2 * r, 0)
            if NFG % 2 == 0:
                f_trans(NFG - 1, 1)
                f_gelu(NFG - 1, 1)

        @block.tensor
        def _(pe):
            pe.wait_ge(consts, 1)
            for s in (hist_free, ch_free):
                pe.sem_inc(s, 4)

            def rank_pass(k, n, w):
                with pe.Fori(0, 8) as i:
                    for u in range(2):
                        pe.wait_ge(sort_oh, i * 2 + (u + 17 * k + 1))
                        pe.matmul(rank_ps[u][0][0:n, 0:w], from_here[0:n, 0:n], onehot[0:n, u, 0:w],
                                  start=True, stop=True)
                        pe.matmul(rank_ps[u][1][0:n, 0:w], ones_b[0:n, 0:n], onehot[0:n, u, 0:w],
                                  start=True, stop=True).then_inc(sort_mm, 1)
                pe.wait_ge(pos_ready, k + 1)

            def turn_list(k, parts):
                pe.wait_ge(list_f, k)
                for s, dest in parts:
                    for b in range(4):
                        last = pe.transpose(dest[:, b * JB:(b + 1) * JB], s[:, b, :], ident[0:JB, 0:JB])
                last.then_inc(list_t, 1)

            def split_product(ps, terms):
                steps = [(a, b, k) for k in terms for a, b in ((0, 0), (0, 1), (1, 0))]
                for n, (a, b, (lhs, rhs)) in enumerate(steps):
                    last = pe.matmul(ps, lhs(a), rhs(b), start=(n == 0), stop=(n == len(steps) - 1))
                return last

            def a_trans(g, u, k):
                n = u * G + k
                if k == 0:
                    pe.wait_ge(a_h, g + 1)
                pe.wait_ge(a_ht, 3 * g + k + 1)
                for c in range(KT):
                    last = pe.transpose(tp_ps[n % 2][:, c * P:(c + 1) * P],
                                        h[:, u, k, c * P:(c + 1) * P], ident[:, :])
                last.then_inc(a_tp, 1)

            def a_proj(g, u, k):
                pe.wait_ge(a_ht, 3 * g + k + 3)
                pe.wait_ge(a_ev, 3 * g + k + 1)
                ps = qkv_ps[(u * G + k) % 2]
                for a, b in ((0, 2 * D), (2 * D, 3 * D)):
                    last = split_product(ps[:, a:b],
                                         [(lambda s, c=c: ht2[:, u, s, k, c * P:(c + 1) * P],
                                           lambda s, c=c: wqkv[:, s, c, a:b]) for c in range(KT)])
                last.then_inc(a_mm, 1)

            def a_group(i, u):
                g = 2 * i + u
                for k in range(G):
                    a_proj(g, u, k)
                    a_trans(g + 1, 1 - u, k)

            def a_loop(lo, hi):
                with pe.Fori(lo, hi) as i:
                    for u in range(2):
                        a_group(i, u)

            rank_pass(0, EP, EC)
            for k in range(G):
                a_trans(0, 0, k)
            pe.wait_ge(wqkv_lo, 1)
            a_loop(cuts[0], cuts[1])
            hist = sort_ps[0][:, 0:LO]
            pe.matmul(hist, zeros_b[0:EP, 0:P], zeros_b[0:EP, :], start=True, stop=False)
            with pe.Fori(0, EC // 4) as i:
                for k in range(4):
                    pe.wait_ge(hist_oh, i * 4 + k + 1)
                    pe.matmul(hist, oh_hi[:, k, :], oh_lo[:, k, :], start=False, stop=False)\
                        .then_inc(hist_free, 1)
            pe.matmul(hist, zeros_b[0:EP, 0:P], zeros_b[0:EP, :], start=False, stop=True)\
                .then_inc(hist_done, 1)

            for p, (lo, hi) in enumerate(((cuts[1], cuts[2]), (cuts[2], cuts[3]), (cuts[3], NGRP // 2))):
                turn_list(p + 1, ((lst_f[:, 0], sort_ps[0]), (lst_f[:, 1], sort_ps[1])))
                rank_pass(p + 1, P, JC)
                a_loop(lo, hi)
            for k in range(G):
                a_proj(NGRP, 0, k)
            turn_list(4, ((lst_f[:, 0], sort_ps[0]), (lst_f[:, 1], sort_ps[1]),
                          (near_f[:, 0], tp_ps[0]), (near_f[:, 1], tp_ps[1])))

            pe.wait_ge(groups_ready, 1)
            groups = pe.value_load(groups_i[0:1, 0:1], min_val=1, max_val=JC // 8)
            pe.wait_ge(cols_ready, 1)

            def turn_scores(c):
                pe.wait_ge(e_smax, c + 1)
                pe.transpose(half[0][0:HEADS, 0:P], smax[:, :], ident[:, :]).then_inc(e_st, 1)

            turn_scores(0)
            with pe.Fori(0, groups * 4) as i:
                for u in range(2):
                    c = i * 2 + u
                    pe.wait_ge(e_state, c + 1)
                    pe.matmul(half[3][:, 0:2 * HEADS + D], carrym[:, u, :], state[:, 1 - u, :],
                              start=True, stop=True)
                    pe.wait_ge(e_run, c + 3)
                    pe.sem_inc(aside, 1)
                    pe.transpose(half[1][:, 0:HEADS], run[:, u, :], ident[0:HEADS, 0:HEADS])\
                        .then_inc(e_rt, 1)
                    pe.wait_ge(e_runt, c + 1)
                    pe.matmul(half[2][:, 0:HEADS], lastm[:, u, :], runt[:, :], start=True, stop=True)\
                        .then_inc(e_max, 1)
                    pe.wait_ge(e_pv, c + 1)
                    pe.matmul(tp_ps[0][:, 0:D + HEADS], same[:, u, :], pv[:, :], start=True, stop=True)\
                        .then_inc(e_sum, 1)
                    turn_scores(c + 1)

            def b_trans(g, i, u, k):
                if k == 0:
                    pe.wait_ge(b_in[u], 16 * i + 16)
                pe.wait_ge(b_at, 3 * g + k + 1)
                for c in range(KT):
                    last = pe.transpose(b_tp_ps[k][:, c * P:(c + 1) * P],
                                        ag[:, u, k, c * P:(c + 1) * P], ident[:, :])
                last.then_inc(b_tp, 1)

            def b_proj(g, u, k):
                pe.wait_ge(b_at, 3 * g + k + 4)
                pe.wait_ge(b_x1t, 3 * g + k + 1)
                for c in range(KT):
                    last = pe.matmul(half[k][:, 0:D], ht[:, u, k, c * P:(c + 1) * P], wo[:, c, :],
                                     start=(c == 0), stop=(c == KT - 1))
                last.then_inc(b_mm, 1)

            pe.wait_ge(late_in, 96)
            for k in range(G):
                b_trans(0, 0, 0, k)
            for k in range(G):
                b_proj(0, 0, k)
                b_trans(1, 0, 1, k)
            with pe.Fori(0, NGRP // 2 - 1) as i:
                for u in range(2):
                    for k in range(G):
                        b_proj(i * 2 + (u + 1), 1 - u, k)
                        b_trans(i * 2 + (u + 2), i + 1, u, k)
            for k in range(G):
                b_proj(NGRP - 1, 1, k)
                b_trans(NGRP, NGRP // 2, 0, k)
            for k in range(G):
                b_proj(NGRP, 0, k)

            with pe.Fori(0, 32) as s:
                pe.wait_ge(t_cnt, s + 1)
                pe.matmul(half[1][:, 0:1], ones[:, :], cntc[:, :], start=True, stop=True)\
                    .then_inc(t_sum, 1)
            for s, m in ((32, ones), (33, before), (34, before), (35, ones), (36, before)):
                pe.wait_ge(t_cnt, s + 1)
                pe.matmul(half[1][:, 0:1], m[:, :], cntc[:, :], start=True, stop=True)\
                    .then_inc(t_sum, 1)

            def list_column(k, wait, **flags):
                pe.wait_ge(ch_oh, wait)
                for s in range(2):
                    last = pe.matmul(sort_ps[s][:, 0:FC], oh_slot[:, k, s, :], oh_col[:, k, :], **flags)
                last.then_inc(ch_free, 1)

            for s in range(2):
                pe.matmul(sort_ps[s][:, 0:FC], zeros_b[:, 0:P], zeros_b[:, 0:FC], start=True, stop=False)
            with pe.Fori(0, T // 4) as i:
                for k in range(4):
                    list_column(k, i * 4 + k + 1, start=False, stop=False)
            for k in range(T // 4 * 4, T):
                list_column(k % 4, k + 1, start=False, stop=False)
            list_column(T % 4, T + 1, start=False, stop=True)
            pe.drain().then_inc(ch_done, 1)

            def f_trans(g, u):
                pe.wait_ge(f_z, g + 1)
                for c in range(FG):
                    pe.wait_ge(f_zt, FG * g + c + 1)
                    for k in range(KT):
                        last = pe.transpose(tp_ps[c % 2][:, k * P:(k + 1) * P],
                                            fz[:, u, c, k * P:(k + 1) * P], ident[:, :])
                    last.then_inc(f_tp, 1)

            def f_up(g, u):
                pe.wait_ge(f_zt, FG * g + FG + 2)
                for k in range(HT):
                    pe.wait_ge(f_h, HT * g + k + 1)
                    split_product(up_ps[k % 4],
                                  [(lambda s, c=c: w1s[:, s, c, k * P:(k + 1) * P],
                                    lambda s, c=c: fzt[:, u, s, c, :]) for c in range(KT)])\
                        .then_inc(f_m1, 1)

            def f_down(g, u, c):
                pe.wait_ge(f_y, FG * g + c + 1)
                split_product(half[2 + c % 2][:, 0:D],
                              [(lambda s, k=k: fh[:, u, s, k, c * P:(c + 1) * P],
                                lambda s, k=k: w2s[:, s, k, :]) for k in range(HT)]).then_inc(f_m2, 1)

            def f_group(g, u, ahead=True):
                f_up(g, u)
                pe.wait_ge(f_h, HT * g + HT + 4)
                f_down(g, u, 0)
                f_down(g, u, 1)
                if ahead:
                    f_trans(g + 1, 1 - u)
                f_down(g, u, 2)
                f_down(g, u, 3)

            pe.wait_ge(w_lo, 2)
            f_trans(0, 0)
            r = (NFG - 1) // 2
            with pe.Fori(0, r) as i:
                for u in range(2):
                    f_group(i * 2 + u, u)
            f_group(2 * r, 0, ahead=NFG % 2 == 0)
            if NFG % 2 == 0:
                f_group(NFG - 1, 1, ahead=False)

        @block.vector
        def _(dve):
            for s in (a_ht, a_ev, b_x1, f_y, f_zt):
                dve.sem_inc(s, 2)
            dve.sem_inc(b_x1t, 3)
            dve.sem_inc(f_h, 4)
            for s in e_out:
                dve.sem_inc(s, 1)
            dve.memset(state[:], 0.0)
            dve.memset(run[:], -BIG)
            dve.memset(idx_all[:], NONE)
            dve.memset(col_row[:], NONE)
            dve.memset(col_last[:], 0.0)
            dve.sem_inc(e_run, 2)
            dve.memset(col_carry[:], -1.0)
            dve.drain().then_inc(e_state, 1)

            dve.wait_ge(edges_in, 32)
            dve.tensor_copy(edge_f[:, :, :], edge[:, :, :])
            dve.tensor_scalar(lo_i[:, :], edge[:, 0, :], LO - 1, None, ALU.bitwise_and)
            dve.tensor_scalar(hi_i[:, :], edge[:, 0, :], LO.bit_length() - 1, None, ALU.logical_shift_right)
            for k in range(2):
                dve.tensor_copy(pay[0:EP, 0:EC, k], edge[:, k, :])
            dve.drain()
            dve.tensor_tensor(is_self[:, :], edge_f[:, 0, :], edge_f[:, 1, :], ALU.is_equal)
            dve.tensor_copy(lo_f[:, :], lo_i[:, :])
            dve.tensor_copy(hi_f[:, :], hi_i[:, :])
            dve.drain()
            dve.scalar_tensor_tensor(lo_f[:, :], lo_f[:, :], 1.0, is_self[:, :], ALU.add, ALU.mult)
            dve.drain()
            dve.tensor_scalar(lo_f[:, :], lo_f[:, :], -1.0, None, ALU.add)
            dve.drain()
            def rank_pass(k, n, w):
                def mark(d, u):
                    dve.tensor_scalar(onehot[0:n, u, 0:w], digit[0:n, 0:w], digits[0:n, ds(d, 1)], None,
                                      ALU.is_equal).then_inc(sort_oh, 1)

                dve.memset(base[:, :], float(LBASE))
                dve.memset(pos[0:n, 0:w], FAR)
                dve.drain()
                mark(0, 0)
                with dve.Fori(0, 8) as i:
                    for u in range(2):
                        dve.wait_ge(sort_mm, i * 2 + (u + 16 * k + 1))
                        dve.tensor_tensor_scan(upto[0:n, 0:w], rank_ps[u][1][0:n, 0:w], zeros[0:n, 0:w],
                                               base[0:n, 0:1], ALU.add, ALU.add)
                        dve.drain()
                        mark(i * 2 + (u + 1), 1 - u)
                        dve.tensor_tensor(place[0:n, 0:w], upto[0:n, 0:w], rank_ps[u][0][0:n, 0:w], ALU.add)
                        dve.tensor_copy(base[0:n, :], upto[0:n, w - 1:w])
                        dve.drain()
                        dve.copy_predicated(pos[0:n, 0:w], onehot[0:n, u, 0:w].bitcast(u16),
                                            place[0:n, 0:w])
                dve.drain()
                dve.tensor_copy(pos_i[0:n, 0:w], pos[0:n, 0:w]).then_inc(pos_ready, 1)

            def list_floats(k):
                dve.wait_ge(list_in, 16 * k + (32 if k == 4 else 0))
                for s in range(2):
                    dve.tensor_copy(lst_f[:, s, :, :],
                                    lst[:, :, :].rearrange("j b (e k) -> j b e k", k=2)[:, :, :, s])
                    if k == 4:
                        dve.tensor_copy(near_f[:, s, :, :],
                                        near[:, s, :, :].rearrange("j b (e k) -> j b e k", k=2)[:, :, :, 0])
                dve.drain().then_inc(list_f, 1)
                dve.wait_ge(list_t, k)

            def list_pass(k):
                list_floats(k)
                dve.tensor_copy(row_i[:, :], sort_ps[0][:, 0:JC])
                dve.tensor_copy(pay[:, 0:JC, 0], sort_ps[0][:, 0:JC])
                dve.tensor_copy(pay[:, 0:JC, 1], sort_ps[1][:, 0:JC])
                dve.drain()
                dve.tensor_scalar(digit_i[:, 0:JC], row_i[:, :], 4 * k, 15, ALU.logical_shift_right,
                                  ALU.bitwise_and)
                dve.drain()
                dve.tensor_copy(digit[:, 0:JC], digit_i[:, 0:JC])
                dve.drain()
                rank_pass(k, P, JC)

            dve.tensor_scalar(digit_i[0:EP, 0:EC], edge[:, 0, :], 15, None, ALU.bitwise_and)
            dve.drain()
            dve.wait_ge(consts, 1)
            dve.scalar_tensor_tensor(digit[0:EP, 0:EC], is_self[:, :], 16.0, digit_i[0:EP, 0:EC],
                                     ALU.mult, ALU.add)
            dve.drain()
            rank_pass(0, EP, EC)
            dve.tensor_scalar(groups_f[0:1, :], base[0:1, :], -float(LBASE), 1.0, ALU.add, ALU.max)
            dve.drain()
            dve.tensor_scalar(groups_i[0:1, :], groups_f[0:1, :], 8.0 * P - 1, None, ALU.add)
            dve.drain()
            dve.tensor_scalar(groups_i[0:1, :], groups_i[0:1, :], (8 * P).bit_length() - 1, None,
                              ALU.logical_shift_right).then_inc(groups_ready, 1)

            def a_stats(g, i, u):
                dve.wait_ge(ax_in[u], 16 * i + 16)
                for k in range(G):
                    dve.bn_stats(stats[:, u, k, :], xg[:, u, k, :])
                dve.drain()
                for k in range(G):
                    last = dve.bn_aggr(mv[:, u, k, :], stats[:, u, k, :])
                last.then_inc(a_var, 1)

            def a_norm(g, u):
                dve.wait_ge(a_sd, g + 1)
                dve.reciprocal(rs[:, u, :], sd[:, u, :])
                dve.drain()
                for k in range(G):
                    last = dve.tensor_scalar(h[:, u, k, :], xg[:, u, k, :], mv[:, u, k, 0:1],
                                             rs[:, u, k:k + 1], ALU.subtract, ALU.mult)
                last.then_inc(a_h, 1)

            def a_low(g, u, k):
                dve.wait_ge(a_hi, 3 * g + k + 1)
                dve.tensor_tensor(ht2[:, u, 1, k, :], tp_ps[(u * G + k) % 2][:, 0:D], ht2[:, u, 0, k, :],
                                  ALU.subtract).then_inc(a_ht, 1)

            def a_evac(g, u, k):
                dve.wait_ge(a_mm, 3 * g + k + 1)
                dve.scalar_tensor_tensor(qkv[:, u, k, :], qkv_ps[(u * G + k) % 2][:, 0:3 * D], 1 / WS,
                                         bqkv[:, :], ALU.mult, ALU.add).then_inc(a_ev, 1)

            def a_group(i, u, ahead=True):
                g = 2 * i + u
                dve.wait_ge(a_stored[u], 32 * i + 16)
                a_evac(g, u, 0)
                if ahead:
                    a_stats(g + 2, i + 1, u)
                a_low(g + 1, 1 - u, 0)
                a_evac(g, u, 1)
                a_low(g + 1, 1 - u, 1)
                if ahead:
                    a_norm(g + 2, u)
                a_evac(g, u, 2)
                a_low(g + 1, 1 - u, 2)

            def a_loop(lo, hi):
                with dve.Fori(lo, hi) as i:
                    for u in range(2):
                        a_group(i, u)

            dve.wait_ge(wqkv_hi, 1)
            dve.scalar_tensor_tensor(wqkv[:, 1, :, :], wqkv_f[:, :, :], WS, wqkv[:, 0, :, :],
                                     ALU.mult, ALU.subtract).then_inc(wqkv_lo, 1)
            dve.wait_ge(consts, 1)
            for u in range(2):
                a_stats(u, 0, u)
                a_norm(u, u)
            for k in range(G):
                a_low(0, 0, k)
            a_loop(cuts[0], cuts[1])

            with dve.Fori(0, EC // 4) as i:
                for k in range(4):
                    dve.wait_ge(hist_free, i * 4 + k + 1)
                    dve.tensor_scalar(oh_hi[:, k, :], iota[0:EP, 0:P], hi_f[:, ds(i * 4 + k, 1)], None,
                                      ALU.is_equal)
                    dve.tensor_scalar(oh_lo[:, k, :], iota[0:EP, :], lo_f[:, ds(i * 4 + k, 1)], None,
                                      ALU.is_equal).then_inc(hist_oh, 1)
            dve.wait_ge(hist_done, 1)
            dve.tensor_copy(cnt_s[:, :], sort_ps[0][0:HI, 0:LO]).then_inc(cnt_ready, 1)

            list_pass(1)
            a_loop(cuts[1], cuts[2])
            list_pass(2)
            a_loop(cuts[2], cuts[3])
            list_pass(3)
            a_loop(cuts[3], NGRP // 2 - 1)
            a_group(NGRP // 2 - 1, 0)
            a_group(NGRP // 2 - 1, 1, ahead=False)
            dve.wait_ge(a_stored[0], 32 * (NGRP // 2) + 16)
            for k in range(G):
                a_evac(NGRP, 0, k)

            list_floats(4)
            row_ps, col_ps, prev_ps, next_ps = [b[:, 0:JC] for b in (*sort_ps, *tp_ps)]
            dve.tensor_copy(col_row[:, 0:JC], row_ps)
            dve.tensor_copy(col_next[:, 0:JC], next_ps)
            dve.tensor_copy(idx_all[:, 0:JC, 0], row_ps)
            dve.tensor_copy(idx_all[:, 0:JC, 1], col_ps)
            dve.tensor_tensor(reset_s[:, :, :], lst_f[:, 0, :, :], near_f[:, 0, :, :], ALU.not_equal)
            dve.drain()
            dve.tensor_scalar(reset_s[:, :, :], reset_s[:, :, :], -BIG, None, ALU.mult).then_inc(reset_ready, 1)
            dve.tensor_tensor(col_last[:, 0:JC], col_row[:, 0:JC], col_next[:, 0:JC], ALU.not_equal)
            dve.tensor_tensor(col_next[:, 0:JC], col_row[:, 0:JC], col_next[:, 0:JC], ALU.is_equal)
            dve.drain()
            dve.scalar_tensor_tensor(col_next[:, 0:JC], col_next[:, 0:JC], FAR, col_row[:, 0:JC],
                                     ALU.mult, ALU.add)
            dve.tensor_scalar(col_last[:, 0:JC], col_last[:, 0:JC], ident[:, P - 1:P], None, ALU.max)
            dve.tensor_scalar(col_carry[:, 1:JC + 1], col_row[:, 0:JC], 1.0, ident[:, P - 1:P],
                              ALU.add, ALU.mult)
            dve.drain()
            dve.tensor_copy(idx_all[:, 0:JC, 2], col_next[:, 0:JC])
            dve.tensor_scalar(col_carry[:, 1:JC + 1], col_carry[:, 1:JC + 1], -1.0, None, ALU.add)
            dve.drain().then_inc(cols_ready, 1)

            groups = dve.value_load(groups_i[0:1, 0:1], min_val=1, max_val=JC // 8)

            def heads(t):
                return t.rearrange("p (h d) -> p h d", h=HEADS)

            def over_heads(t):
                return t.unsqueeze(2).to_broadcast([P, HEADS, HD])

            def scores(c, i, u):
                dve.wait_ge(e_row_in[u], 32 * i + 32)
                dve.wait_ge(e_in[u], 48 * i + 48)
                q, k_row, k_col = rowg[:, u, 0:D], rowg[:, u, D:2 * D], colg[:, u, D:2 * D]
                row = col_row[:, ds(c, 1)]
                dve.tensor_tensor(qk[:, 0, :], q, k_col, ALU.mult)
                dve.tensor_tensor(qk[:, 1, :], q, k_row, ALU.mult)
                dve.tensor_scalar(same[:, u, :], row_bc[:, u, :, 0], row, None, ALU.is_equal)
                dve.tensor_scalar(lastm[:, u, :], row_bc[:, u, :, 0], row, col_last[:, ds(c, 1)],
                                  ALU.is_equal, ALU.mult)
                dve.tensor_scalar(carrym[:, u, :], row_bc[:, u, :, 0], col_carry[:, ds(c, 1)], None,
                                  ALU.is_equal)
                dve.tensor_scalar(no_self[:, :], cntg[:, u, :], 0.0, -BIG, ALU.is_equal, ALU.mult)
                dve.drain()
                dve.tensor_reduce(raw[:, :, :], qk[:, :, :].rearrange("p s (h d) -> p s h d", h=HEADS),
                                  AX, ALU.add)
                dve.drain()
                dve.tensor_scalar(sc[:, u, 0, :], raw[:, 0, :], SCALE, None, ALU.mult)
                dve.tensor_scalar(sc[:, u, 1, :], raw[:, 1, :], SCALE, no_self[:, :], ALU.mult, ALU.add)
                dve.drain()
                dve.tensor_tensor(smax[:, :], sc[:, u, 0, :], sc[:, u, 1, :], ALU.max).then_inc(e_smax, 1)

            scores(0, 0, 0)
            with dve.Fori(0, groups * 4) as i:
                for u in range(2):
                    c = i * 2 + u
                    v_row, v_col = rowg[:, u, 2 * D:], colg[:, u, 2 * D:]
                    dve.wait_ge(e_st, c + 1)
                    dve.tensor_tensor_scan(run[:, u, :], reset_bc[:, u, :], half[0][0:HEADS, 0:P],
                                           run[:, 1 - u, P - 1:P], ALU.add, ALU.max).then_inc(e_run, 1)
                    dve.wait_ge(e_cmax, c + 1)
                    top = state[:, u, 0:HEADS]
                    dve.tensor_tensor(expo[:, 0, :], sc[:, u, 0, :], top, ALU.subtract)
                    dve.tensor_tensor(expo[:, 1, :], sc[:, u, 1, :], top, ALU.subtract)
                    dve.tensor_tensor(expo[:, 2, :], half[3][:, 0:HEADS], top, ALU.subtract)
                    dve.drain()
                    dve.tensor_scalar(expo[:, :, :], expo[:, :, :], 0.0, None, ALU.min).then_inc(e_expo, 1)
                    dve.wait_ge(e_ex, c + 1)
                    dve.tensor_tensor(heads(pv[:, 0:D]), heads(v_col), over_heads(ex[:, 0, :]), ALU.mult)
                    dve.tensor_copy(pv[:, D:D + HEADS], ex[:, 0, :]).then_inc(e_pv, 1)
                    dve.tensor_scalar(selfw[:, :], ex[:, 1, :], cntg[:, u, :], None, ALU.mult)
                    dve.tensor_tensor(heads(carried[:, 0:D]), heads(half[3][:, HEADS:HEADS + D]),
                                      over_heads(ex[:, 2, :]), ALU.mult)
                    dve.tensor_tensor(carried[:, D:], half[3][:, HEADS + D:2 * HEADS + D], ex[:, 2, :],
                                      ALU.mult)
                    dve.drain()
                    dve.tensor_tensor(heads(selfv[:, :]), heads(v_row), over_heads(selfw[:, :]), ALU.mult)\
                        .then_inc(e_used, 1)
                    scores(c + 1, i + u, 1 - u)
                    dve.wait_ge(e_sum, c + 1)
                    dve.tensor_tensor(state[:, u, HEADS:], tp_ps[0][:, 0:D + HEADS], carried[:, :], ALU.add)\
                        .then_inc(e_state, 1)
                    dve.drain()
                    dve.tensor_tensor(tot[:, :], state[:, u, HEADS:HEADS + D], selfv[:, :], ALU.add)
                    dve.tensor_tensor(totw[:, :], state[:, u, HEADS + D:], selfw[:, :], ALU.add)
                    dve.drain()
                    dve.reciprocal(totw[:, :], totw[:, :])
                    dve.drain()
                    dve.wait_ge(e_sc[u], 32 * i + 16)
                    dve.tensor_tensor(heads(outb[:, u, :]), heads(tot[:, :]), over_heads(totw[:, :]),
                                      ALU.mult).then_inc(e_out[u], 1)

            for n, (whole, parts) in enumerate(((w1f, w1s), (w2f, w2s))):
                dve.wait_ge(w_hi, n + 1)
                dve.scalar_tensor_tensor(parts[:, 1, :, :], whole[:, :, :], WS, parts[:, 0, :, :],
                                         ALU.mult, ALU.subtract).then_inc(w_lo, 1)

            dve.wait_ge(has_in, 64)
            dve.tensor_tensor(has[:, :], cnt_n[:, :], seen_n[:, :], ALU.add)
            dve.drain()
            dve.tensor_scalar(has[:, :], has[:, :], 0.0, None, ALU.is_gt)
            dve.wait_ge(late_in, 96)
            dve.drain()

            def b_x(g, u):
                dve.wait_ge(b_xb, g + 1)
                dve.wait_ge(b_u, g + 1)
                for k in range(G):
                    dve.wait_ge(b_mm, 3 * g + k + 1)
                    last = dve.scalar_tensor_tensor(x1[:, u, k, :], half[k][:, 0:D],
                                                    has[:, ds(g * G + k, 1)], xb[:, u, k, :],
                                                    ALU.mult, ALU.add)
                    last.then_inc(b_x1t, 1)

            def b_stats(u):
                for k in range(G):
                    dve.bn_stats(stats[:, u, k, :], x1[:, u, k, :])

            def b_aggr(u):
                for k in range(G):
                    last = dve.bn_aggr(mv[:, u, k, :], stats[:, u, k, :])
                last.then_inc(b_var, 1)

            def b_dots(g, u):
                dve.wait_ge(b_z, g + 1)
                for k in range(G):
                    dve.tensor_tensor_reduce(out=zt[:, 1 - u, k, :], in0=zt[:, 1 - u, k, :], in1=wrs[:, :],
                                             scale=1.0, scalar=0.0, op0=ALU.mult, op1=ALU.add,
                                             accum_out=wst[:, 1 - u, k:k + 1])

            def b_step(g, u, ahead=True):
                if ahead:
                    b_x(g + 1, 1 - u)
                dve.wait_ge(b_sd, g + 1)
                dve.reciprocal(rs[:, u, :], sd[:, u, :])
                if ahead:
                    dve.drain().then_inc(b_x1, 1)
                else:
                    dve.drain()
                dve.tensor_copy(weight_at[:, ds(g * G, G)], wst[:, u, :])
                dve.tensor_scalar(gain[:, u, :], rs[:, u, :], 1.0, None, ALU.add)
                dve.scalar_tensor_tensor(shift[:, u, :], mv[:, u, :, 0], -1.0, rs[:, u, :], ALU.mult, ALU.mult)\
                    .then_inc(b_gain, 1)
                if ahead:
                    b_stats(1 - u)
                    dve.drain()
                    b_aggr(1 - u)
                b_dots(g, u)
                dve.tensor_copy(rs_n[:, ds(g * G, G)], rs[:, u, :])
                dve.tensor_copy(mean_n[:, ds(g * G, G)], mv[:, u, :, 0])

            b_x(0, 0)
            dve.memset(wst[:], 0.0)
            dve.memset(zt[:, 1], 0.0)
            dve.drain().then_inc(b_x1, 1)
            b_stats(0)
            dve.drain()
            b_aggr(0)
            with dve.Fori(0, NGRP // 2) as i:
                b_step(i * 2, 0)
                b_step(i * 2 + 1, 1)
            b_step(NGRP, 0, ahead=False)
            dve.drain()
            dve.tensor_copy(weight[:, (NGRP - 1) * G:NGRP * G], wst[:, 1, :])
            b_dots(NGRP + 1, 1)
            dve.drain()
            dve.tensor_copy(weight[:, NGRP * G:TC], wst[:, 0, :])
            dve.drain()

            dve.tensor_scalar(weight[:, :], weight[:, :], brs[:, 0:1], None, ALU.add)
            dve.tensor_scalar(has[:, :], rs_n[:, :], 1.0, None, ALU.add)
            dve.drain()
            dve.reciprocal(has[:, :], has[:, :])
            for k in (2, 3):
                dve.tensor_copy(norm_s[:, :, k], weight[:, :])
            dve.drain()
            dve.tensor_tensor(norm_s[:, :, 0], has[:, :], rs_n[:, :], ALU.mult)
            dve.drain()
            dve.scalar_tensor_tensor(norm_s[:, :, 1], mean_n[:, :], -1.0, norm_s[:, :, 0], ALU.mult, ALU.mult)
            dve.drain().then_inc(norm_ready, 1)

            wbits = weight[:, 0:T + 1].bitcast(i32)
            dve.tensor_scalar(key_a[:, :], wbits, 31, -2 ** 31, ALU.arith_shift_right, ALU.bitwise_or)
            dve.drain()
            dve.tensor_tensor(key_b[:, :], wbits, key_a[:, :], ALU.bitwise_xor)
            dve.drain()
            dve.tensor_scalar(key_a[:, :], key_b[:, :], 16, 65535, ALU.logical_shift_right, ALU.bitwise_and)
            dve.tensor_scalar(key_b[:, :], key_b[:, :], 65535, None, ALU.bitwise_and)
            dve.drain()
            dve.tensor_copy(key[:, 0, :], key_a[:, :])
            dve.tensor_copy(key[:, 1, :], key_b[:, :])
            dve.memset(thr[:, :], 0.0)
            dve.drain()
            for k in range(2):
                dve.tensor_scalar(key[:, k, T:T + 1], key[:, k, T:T + 1], 1.0, live[:, :], ALU.add, ALU.mult)
            dve.drain()
            for k in range(2):
                dve.tensor_scalar(key[:, k, T:T + 1], key[:, k, T:T + 1], -1.0, None, ALU.add)
            dve.drain()

            def largest(level, keys):
                t = thr[:, level:level + 1]
                with dve.Fori(0, 16) as s:
                    dve.tensor_scalar(cand[:, :], t, bits[:, ds(s, 1)], None, ALU.add)
                    dve.drain()
                    dve.tensor_scalar(hit[:, :], keys, cand[:, 0:1], None, ALU.is_ge, ALU.add,
                                      accum_out=cntc[:, :])
                    dve.drain().then_inc(t_cnt, 1)
                    dve.wait_ge(t_sum, s + (16 * level + 1))
                    dve.tensor_scalar(step[:, :], half[1][:, 0:1], KK - 0.5, bits[:, ds(s, 1)],
                                      ALU.is_gt, ALU.mult)
                    dve.drain()
                    dve.tensor_tensor(t, t, step[:, :], ALU.add)
                    dve.drain()

            largest(0, key[:, 0, :])
            dve.tensor_scalar(hit[:, :], key[:, 0, :], thr[:, 0:1], FAR + 1, ALU.is_gt, ALU.mult)
            dve.tensor_scalar(tied[:, :], key[:, 0, :], thr[:, 0:1], None, ALU.is_equal)
            dve.tensor_scalar(key[:, 1, :], key[:, 1, :], 1.0, None, ALU.add)
            dve.drain()
            dve.tensor_tensor(keyl[:, :], tied[:, :], key[:, 1, :], ALU.mult)
            dve.drain()
            dve.scalar_tensor_tensor(keyl[:, :], keyl[:, :], -1.0, hit[:, :], ALU.add, ALU.add)
            dve.drain()
            largest(1, keyl[:, :])

            def summed(n, column):
                dve.tensor_copy(cntc[:, :], column)
                dve.drain().then_inc(t_cnt, 1)
                dve.wait_ge(t_sum, n + 1)
                return half[1][:, 0:1]

            dve.tensor_scalar(hit[:, :], keyl[:, :], thr[:, 1:2], None, ALU.is_gt, ALU.add,
                              accum_out=step[:, :])
            dve.tensor_scalar(tied[:, :], keyl[:, :], thr[:, 1:2], None, ALU.is_equal)
            dve.drain()
            dve.tensor_scalar(need[:, :], summed(32, step[:, :]), -1.0, float(KK), ALU.mult, ALU.add)
            dve.tensor_tensor_scan(rank[:, 0:T], tied[:, 0:T], zeros[:, 0:T], 0.0, ALU.add, ALU.add)
            dve.drain()
            dve.tensor_copy(step[:, :], rank[:, T - 1:T])
            dve.drain()
            dve.tensor_copy(off[:, 0:1], summed(33, step[:, :]))
            dve.tensor_copy(off[:, 1:2], summed(34, tied[:, T:T + 1]))
            dve.tensor_copy(off1[:, :], summed(35, step[:, :]))
            dve.drain()
            dve.scalar_tensor_tensor(rank[:, 0:T], rank[:, 0:T], off[:, 0:1], tied[:, 0:T],
                                     ALU.add, ALU.subtract)
            dve.tensor_tensor(rank[:, T:T + 1], off[:, 1:2], off1[:, :], ALU.add)
            dve.drain()
            dve.scalar_tensor_tensor(tied[:, :], rank[:, :], need[:, 0:1], tied[:, :], ALU.is_lt, ALU.mult)
            dve.drain()
            dve.tensor_tensor(hit[:, :], hit[:, :], tied[:, :], ALU.add)
            dve.drain()
            dve.tensor_tensor_scan(rank[:, :], hit[:, :], zeros[:, 0:T + 1], 0.0, ALU.add, ALU.add)
            dve.drain()
            dve.tensor_copy(off[:, 0:1], summed(36, rank[:, T:T + 1]))
            dve.drain()
            dve.scalar_tensor_tensor(rank[:, :], rank[:, :], off[:, 0:1], hit[:, :], ALU.add, ALU.subtract)
            dve.drain()
            dve.scalar_tensor_tensor(rank[:, :], rank[:, :], -FAR, hit[:, :], ALU.add, ALU.mult)
            dve.drain()
            dve.tensor_scalar(chpos[:, :], rank[:, :], FAR, None, ALU.add)
            dve.drain()
            for src_i, dest, n in ((chpos[:, :], slot_f, 7), (node[:, 0:T + 1], node_f, 8)):
                dve.tensor_scalar(key_a[:, :], src_i, (1 << n) - 1, None, ALU.bitwise_and)
                dve.tensor_scalar(key_b[:, :], src_i, n, None, ALU.logical_shift_right)
                dve.drain()
                dve.tensor_copy(dest[:, 0, :], key_a[:, :])
                dve.tensor_copy(dest[:, 1, :], key_b[:, :])
                dve.drain()

            def list_column(k, t, free):
                dve.wait_ge(ch_free, free)
                for s in range(2):
                    dve.tensor_scalar(oh_slot[:, k, s, :], iota[:, 0:P], slot_f[:, 0, t], node_f[:, s, t],
                                      ALU.is_equal, ALU.mult)
                dve.tensor_scalar(oh_col[:, k, :], iota[:, 0:FC], slot_f[:, 1, t], None, ALU.is_equal)\
                    .then_inc(ch_oh, 1)

            with dve.Fori(0, T // 4) as i:
                for k in range(4):
                    list_column(k, ds(i * 4 + k, 1), i * 4 + k + 1)
            for k in range(T // 4 * 4, T + 1):
                list_column(k % 4, slice(k, k + 1), k + 1)
            dve.tensor_scalar(past[:, :], iota[:, 0:FC], float(P), pcol[:, 0:1], ALU.mult, ALU.add)
            dve.drain()
            dve.tensor_scalar(past[:, :], past[:, :], KK - 0.5, FAR, ALU.is_gt, ALU.mult)
            dve.wait_ge(ch_done, 1)
            dve.drain()
            dve.tensor_tensor(past[:, :], sort_ps[0][:, 0:FC], past[:, :], ALU.add)
            dve.drain()
            dve.scalar_tensor_tensor(chosen[:, :], sort_ps[1][:, 0:FC], 256.0, past[:, :], ALU.mult, ALU.add)\
                .then_inc(ch_ready, 1)

            def f_norm(g, i, u):
                dve.wait_ge(f_in[u], 2 * FG * 16 * (i + 1))
                for c in range(FG):
                    last = dve.tensor_scalar(fz[:, u, c, :], fu[:, u, c, :], fn[:, u, c, 0:1],
                                             fn[:, u, c, 1:2], ALU.mult, ALU.add)
                last.then_inc(f_z, 1)

            def f_zlow(g, u):
                for c in range(FG):
                    dve.wait_ge(f_zh, FG * g + c + 1)
                    dve.tensor_tensor(fzt[:, u, 1, :, c * P:(c + 1) * P],
                                      tp_ps[c % 2][:, 0:D].rearrange("p (k n) -> p k n", k=KT),
                                      fzt[:, u, 0, :, c * P:(c + 1) * P], ALU.subtract).then_inc(f_zt, 1)

            def f_hlow(g, u):
                for k in range(HT):
                    dve.wait_ge(f_g, HT * g + k + 1)
                    dve.tensor_tensor(fh[:, u, 1, k, :], up_ps[k % 4], fh[:, u, 0, k, :], ALU.subtract)\
                        .then_inc(f_h, 1)

            def f_out(g, i, u, c):
                if c == 0:
                    dve.wait_ge(f_sc[u], FG * 16 * i + 16)
                dve.wait_ge(f_m2, FG * g + c + 1)
                dve.scalar_tensor_tensor(fy[:, c % 2, :], half[2 + c % 2][:, 0:D], 1 / WS, b2s[:, :],
                                         ALU.mult, ALU.add).then_inc(f_y, 1)
                dve.drain()
                last = dve.scalar_tensor_tensor(fo[:, u, c, :], fy[:, c % 2, :], fn[:, u, c, 2:3],
                                                fu[:, u, c, :], ALU.mult, ALU.add)
                if c == FG - 1:
                    last.then_inc(f_o, 1)

            def f_group(g, i, u, ahead=True):
                f_hlow(g, u)
                if ahead:
                    f_norm(g + 1, i + u, 1 - u)
                f_out(g, i, u, 0)
                f_out(g, i, u, 1)
                if ahead:
                    f_zlow(g + 1, 1 - u)
                f_out(g, i, u, 2)
                f_out(g, i, u, 3)

            f_norm(0, 0, 0)
            f_zlow(0, 0)
            r = (NFG - 1) // 2
            with dve.Fori(0, r) as i:
                for u in range(2):
                    f_group(i * 2 + u, i, u)
            f_group(2 * r, r, 0, ahead=NFG % 2 == 0)
            if NFG % 2 == 0:
                f_group(NFG - 1, r, 1, ahead=False)


_INS = ["x", "src", "dst", "L0_gnn_Wq", "L0_gnn_bq", "L0_gnn_Wk", "L0_gnn_bk", "L0_gnn_Wv", "L0_gnn_bv",
        "L0_gnn_Wo", "L0_gnn_bo", "L0_ffn_wr", "L0_ffn_br", "L0_ffn_w1", "L0_ffn_b1", "L0_ffn_w2",
        "L0_ffn_b2"]


def kernel(**inputs):
    import numpy as np
    import concourse.bacc as bacc
    from concourse.bass_utils import run_bass_kernel_spmd

    nc = bacc.Bacc("TRN2", target_bir_lowering=False, num_devices=1)
    arrays, args = {}, []
    for name in _INS:
        a = np.ascontiguousarray(inputs[name])
        arrays[f"in_{name}"] = a
        args.append(nc.dram_tensor(f"in_{name}", a.shape, mybir.dt.from_np(a.dtype),
                                   kind="ExternalInput").ap())
    shape = arrays["in_x"].shape
    out = nc.dram_tensor("out", shape, f32, kind="ExternalOutput").ap()
    gnn_ffn_kernel(nc, *args, out)
    r = run_bass_kernel_spmd(nc, [arrays], core_ids=[0])
    return r.results[0]["out"]
```
